# Optimizing a Trainium2 kernel written in Bass

```python
import numpy as np
import jax
import jax.numpy as jnp

def _softmax(x, axis=-1):
    return jax.nn.softmax(x, axis=axis)

def _gelu(x):
    return jax.nn.gelu(x, approximate=True)

def _silu(x):
    return jax.nn.silu(x)

def _sigmoid(x):
    return jax.nn.sigmoid(x)

def _layernorm(x, axis=-1, eps=1e-05):
    m = jnp.mean(x, axis=axis, keepdims=True)
    v = jnp.var(x, axis=axis, keepdims=True)
    return (x - m) / jnp.sqrt(v + eps)

def _scatter_add(tgt, idx, src, axis=0):
    return tgt.at[idx].add(src)

def _segment_sum(src, seg, n):
    return jax.ops.segment_sum(src, seg, n)
kernel_name = 'mk_cond_seq_d1_seqx_r2_b22e02'

def setup_inputs(seed: int=0):
    np.random.seed(seed)
    _w = jnp.asarray

    def _rec_inputs():
        import jax
        import jax.numpy as jnp
        _rk = jax.random.key(seed)
        x = 1.648e-05 + 1 * jax.random.normal(jax.random.fold_in(_rk, 1), (2, 2048, 576), jnp.float32)
        _lenS = 2048 - jax.random.randint(jax.random.fold_in(_rk, 7), (2,), 0, max(1, 2048 // 4) + 1, jnp.int32)
        _lenS2 = 2048 - jax.random.randint(jax.random.fold_in(_rk, 8), (2,), 0, max(1, 2048 // 4) + 1, jnp.int32)
        cond_1152 = 0.00914911 + 1.00357 * jax.random.normal(jax.random.fold_in(_rk, 11), (2, 576), jnp.float32)
        return (x, cond_1152)
    x, cond_1152 = _rec_inputs()

    def _L0_cond_setup():
        import jax, jax.numpy as jnp
        import numpy as np
        B, L, C = (8, 512, 576)
        H = 16
        D = C // H
        FF = int(C * 4.0)
        EPS = 1e-06

        def _layernorm(x):
            mu = jnp.mean(x, axis=-1, keepdims=True)
            var = jnp.mean(jnp.square(x - mu), axis=-1, keepdims=True)
            return (x - mu) * jax.lax.rsqrt(var + EPS)

        def _modulate(x, shift, scale):
            return x * (1.0 + scale) + shift

        def _attention(h, W_qkv, b_qkv, W_proj, b_proj):
            b, l, c = h.shape
            qkv = h @ W_qkv + b_qkv
            qkv = qkv.reshape(b, l, 3, H, D)
            q, k, v = (qkv[:, :, 0], qkv[:, :, 1], qkv[:, :, 2])
            scale = D ** (-0.5)
            scores = jnp.einsum('blhd,bmhd->bhlm', q * scale, k)
            attn = jax.nn.softmax(scores, axis=-1)
            o = jnp.einsum('bhlm,bmhd->blhd', attn, v).reshape(b, l, c)
            return o @ W_proj + b_proj
        key = jax.random.key(seed)
        ks = jax.random.split(key, 12)
        s = 0.02
        return {'x': jax.random.normal(ks[0], (B, L, C), jnp.float32), 'c': jax.random.normal(ks[1], (B, 1, C), jnp.float32), 'W_qkv': jax.random.normal(ks[2], (C, 3 * C), jnp.float32) * s, 'b_qkv': jnp.zeros((3 * C,), jnp.float32), 'W_proj': jax.random.normal(ks[3], (C, C), jnp.float32) * s, 'b_proj': jnp.zeros((C,), jnp.float32), 'W_fc1': jax.random.normal(ks[4], (C, FF), jnp.float32) * s, 'b_fc1': jnp.zeros((FF,), jnp.float32), 'W_fc2': jax.random.normal(ks[5], (FF, C), jnp.float32) * s, 'b_fc2': jnp.zeros((C,), jnp.float32), 'W_ada': jax.random.normal(ks[6], (C, 6 * C), jnp.float32) * s, 'b_ada': jnp.zeros((6 * C,), jnp.float32)}
    _L0_cond_all = _L0_cond_setup()
    _L0_cond_in = {k: v for k, v in _L0_cond_all.items() if k in ('W_qkv', 'b_qkv', 'W_proj', 'b_proj', 'W_fc1', 'b_fc1', 'W_fc2', 'b_fc2', 'W_ada', 'b_ada')}
    del _L0_cond_all
    return {'x': x, 'cond_1152': cond_1152, 'L0_cond_W_qkv': _L0_cond_in['W_qkv'], 'L0_cond_b_qkv': _L0_cond_in['b_qkv'], 'L0_cond_W_proj': _L0_cond_in['W_proj'], 'L0_cond_b_proj': _L0_cond_in['b_proj'], 'L0_cond_W_fc1': _L0_cond_in['W_fc1'], 'L0_cond_b_fc1': _L0_cond_in['b_fc1'], 'L0_cond_W_fc2': _L0_cond_in['W_fc2'], 'L0_cond_b_fc2': _L0_cond_in['b_fc2'], 'L0_cond_W_ada': _L0_cond_in['W_ada'], 'L0_cond_b_ada': _L0_cond_in['b_ada']}

def reference(x, cond_1152, L0_cond_W_qkv, L0_cond_b_qkv, L0_cond_W_proj, L0_cond_b_proj, L0_cond_W_fc1, L0_cond_b_fc1, L0_cond_W_fc2, L0_cond_b_fc2, L0_cond_W_ada, L0_cond_b_ada):
    import jax
    import jax.numpy as jnp

    def _L0_cond_ref(x, c, W_qkv, b_qkv, W_proj, b_proj, W_fc1, b_fc1, W_fc2, b_fc2, W_ada, b_ada):
        import jax, jax.numpy as jnp
        import numpy as np
        B, L, C = (8, 512, 576)
        H = 16
        D = C // H
        FF = int(C * 4.0)
        EPS = 1e-06

        def _layernorm(x):
            mu = jnp.mean(x, axis=-1, keepdims=True)
            var = jnp.mean(jnp.square(x - mu), axis=-1, keepdims=True)
            return (x - mu) * jax.lax.rsqrt(var + EPS)

        def _modulate(x, shift, scale):
            return x * (1.0 + scale) + shift

        def _attention(h, W_qkv, b_qkv, W_proj, b_proj):
            b, l, c = h.shape
            qkv = h @ W_qkv + b_qkv
            qkv = qkv.reshape(b, l, 3, H, D)
            q, k, v = (qkv[:, :, 0], qkv[:, :, 1], qkv[:, :, 2])
            scale = D ** (-0.5)
            scores = jnp.einsum('blhd,bmhd->bhlm', q * scale, k)
            attn = jax.nn.softmax(scores, axis=-1)
            o = jnp.einsum('bhlm,bmhd->blhd', attn, v).reshape(b, l, c)
            return o @ W_proj + b_proj
        ada = jax.nn.silu(c) @ W_ada + b_ada
        shift_msa, scale_msa, gate_msa, shift_mlp, scale_mlp, gate_mlp = jnp.split(ada, 6, axis=-1)
        h = _modulate(_layernorm(x), shift_msa, scale_msa)
        x = x + gate_msa * _attention(h, W_qkv, b_qkv, W_proj, b_proj)
        h = _modulate(_layernorm(x), shift_mlp, scale_mlp)
        mlp = jax.nn.gelu(h @ W_fc1 + b_fc1, approximate=True) @ W_fc2 + b_fc2
        x = x + gate_mlp * mlp
        return x
    x = _L0_cond_ref(x, cond_1152[:, None, :], L0_cond_W_qkv, L0_cond_b_qkv, L0_cond_W_proj, L0_cond_b_proj, L0_cond_W_fc1, L0_cond_b_fc1, L0_cond_W_fc2, L0_cond_b_fc2, L0_cond_W_ada, L0_cond_b_ada)
    return x

_drawn_inputs = setup_inputs


def setup_inputs(seed=0):
    import zlib

    import numpy as np

    out = dict(_drawn_inputs(seed))
    spreads = {'L0_cond_b_qkv': (0.0, 0.61),
     'L0_cond_b_proj': (0.0, 0.1),
     'L0_cond_b_fc1': (0.0, 0.426),
     'L0_cond_b_fc2': (0.0, 0.271),
     'L0_cond_b_ada': (0.0, 0.1)}
    factors = {}
    for name, (base, spread) in spreads.items():
        noise = np.random.default_rng([zlib.crc32(name.encode()), seed]).standard_normal(out[name].shape)
        drawn = base * np.exp(spread * noise) if base else spread * noise
        out[name] = jnp.asarray(drawn.astype(out[name].dtype))
    for name, factor in factors.items():
        out[name] = (out[name] * factor).astype(out[name].dtype)
    return out
```

```python
from contextlib import ExitStack

import numpy as np

import concourse.bass as bass
from concourse import mybir

F = mybir.dt.float32
R = mybir.dt.float32r
ALU = mybir.AluOpType
ACT = mybir.ActivationFunctionType
AX = mybir.AxisListType

B = 2
L = 2048
C = 576
H = 16
D = 36
FF = 2304
T = B * L
EPS = 1e-6
SCALE = float(D) ** -0.5
CH = 512
NCH = T // CH
KT = 5
NF = 2 * C // 128
HALF = C // 2
VW = 64 + D + 1
SPLIT = (0, 2, 3, 5, 7, 8, 10, 11, 13, 15)


class Counter:

    def __init__(self, sem):
        self.sem = sem
        self.n = 0

    def now(self):
        return (self, self.n)


class Queues:

    def __init__(self):
        self.q = {e: [] for e in ("sync", "tensor", "vector", "scalar", "gpsimd")}

    def put(self, eng, fn, waits=(), inc=None, by=1):
        if inc is not None:
            inc.n += by
        self.q[eng].append(([w for w in waits if w is not None], fn, inc, by))
        return inc.now() if inc is not None else None

    def run(self, eng, e):
        seen = {}
        for waits, fn, inc, by in self.q[eng]:
            for c, v in waits:
                if v > 0 and seen.get(c, 0) < v:
                    e.wait_ge(c.sem, v)
                    seen[c] = v
            ins = fn(e)
            if inc is not None:
                ins.then_inc(inc.sem, by)

    def emit(self, nc):
        with nc.Block() as block:
            for name in self.q:
                def body(e, name=name):
                    self.run(name, e)
                blocks = {"sync": block.sync, "tensor": block.tensor, "vector": block.vector,
                                "scalar": block.scalar, "gpsimd": block.gpsimd}
                blocks[name](body)


class Scope:

    def __init__(self, nc, ctx, tag, sems):
        self.nc, self.ctx, self.tag, self.sems = nc, ctx, tag, sems

    def sb(self, name, shape, dt=F):
        return self.ctx.enter_context(self.nc.sbuf_tensor(f"{self.tag}_{name}", shape, dt))

    def ps(self, name, shape):
        return self.ctx.enter_context(self.nc.psum_tensor(f"{self.tag}_{name}", shape, F))

    def sem(self, name):
        return Counter(self.sems.enter_context(self.nc.semaphore(f"{self.tag}_s_{name}")))


def drain(q, counters):
    for c in counters:
        q.q["sync"].append(([c.now()], lambda e: None, None, 0))


def finish(q):
    out = q.q["sync"]
    while out and out[-1][2] is None:
        out.pop()


def split_rows(q, s, W, wh, wl, wm, wr, c0, nc_, stg, s_ld, s_hi, s_lo, s_z, free):
    toks = []
    z = q.put("vector", lambda e: e.memset(wr[64:128, :].bitcast(F), 0.0), (), s_z)
    for kt in range(KT):
        b = kt % 2
        w = stg[b]
        if kt < 4:
            ld = q.put("sync", lambda e, kt=kt, w=w: e.dma_start(w[:, 0:nc_], W[kt * 128:kt * 128 + 128, c0:c0 + nc_]),
                       (free[b],), s_ld[b], 16)
            hi = q.put("scalar", lambda e, kt=kt, w=w: e.activation(wh[:, kt, :], w[:, 0:nc_], ACT.Copy), (ld,), s_hi)
            lo = q.put("vector", lambda e, kt=kt, w=w: e.tensor_tensor(
                wl[:, kt, :], w[:, 0:nc_], wh[:, kt, :].bitcast(F), ALU.subtract), (ld, hi), s_lo)
        else:
            q.put("sync", lambda e, w=w: e.dma_start(w[0:64, 0:nc_], W[512:576, c0:c0 + nc_]), (free[b],), s_ld[b], 16)
            ld = q.put("sync", lambda e, w=w: e.dma_start(w[64:128, 0:nc_], W[512:576, c0:c0 + nc_]), (free[b],),
                       s_ld[b], 16)
            hi = q.put("scalar", lambda e, w=w: e.activation(wm[:, :], w[:, 0:nc_], ACT.Copy), (ld,), s_hi)
            lo = q.put("vector", lambda e, w=w: e.tensor_tensor(
                wr[0:64, :], w[0:64, 0:nc_], wm[0:64, :].bitcast(F), ALU.subtract), (ld, hi), s_lo)
        free[b] = lo
        toks += [lo, hi]
    return [toks[-2], toks[-1], z]


def passes(wh, wl, wm, wr, hh, lo, wsl, tsl):
    out = []
    for kt in range(4):
        out += [(wh[:, kt, wsl], hh[:, kt, tsl]), (wh[:, kt, wsl], lo[:, kt, tsl]), (wl[:, kt, wsl], hh[:, kt, tsl])]
    out += [(wm[:, wsl], hh[:, 4, tsl]), (wr[:, wsl], hh[:, 4, tsl])]
    return out


def passes_t(wh, wl, wm, wr, hh, lo, wsl, tsl):
    out = []
    for kt in range(4):
        out += [(hh[:, kt, tsl], wh[:, kt, wsl]), (hh[:, kt, tsl], wl[:, kt, wsl]), (lo[:, kt, tsl], wh[:, kt, wsl])]
    out += [(hh[:, 4, tsl], wm[:, wsl]), (hh[:, 4, tsl], wr[:, wsl])]
    return out


def program(nc, x, cond, W_qkv, b_qkv, W_proj, b_proj, W_fc1, b_fc1, W_fc2, b_fc2, W_ada, b_ada, out):
    xf = x.rearrange("b l c -> (b l) c")
    of = out.rearrange("b l c -> (b l) c")

    def dram(name, shape):
        return nc.dram_tensor(name, shape, F, kind="Internal").ap()

    qkh = dram("qkh", [2 * C, T])
    qkl = dram("qkl", [2 * C, T])
    vd = dram("vd", [T, H * (D + 1)])
    aod = dram("aod", [T, C])
    hth = dram("hth", [KT, 128, T])
    htl = dram("htl", [4, 128, T])
    y1 = dram("y1", [T, C])
    y2 = dram("y2", [T, C])
    gd = dram("gd", [2, 2, C])

    with ExitStack() as top:
        P = Scope(nc, top, "g", top)
        ident = P.sb("ident", [128, 128])
        adaT = P.sb("adaT", [128, 6, KT, 2])
        eps = P.sb("eps", [128, 1])
        bq = P.sb("bq", [128, NF])

        with ExitStack() as ctx:
            A = Scope(nc, ctx, "a", top)
            wh = A.sb("wh", [128, 4, 3 * C], R)
            wl = A.sb("wl", [128, 4, 3 * C], R)
            wm = A.sb("wm", [128, 3 * C], R)
            wr = A.sb("wr", [128, 3 * C], R)
            phase_setup(nc, P, ident, adaT, eps, bq, gd, wh, wl, wm, wr, cond, W_ada, b_ada, W_qkv, b_qkv)
            phase_qkv(nc, A, ident, adaT, eps, bq, wh, wl, wm, wr, xf, b_qkv, qkh, qkl, vd)
        with ExitStack() as ctx:
            phase_attention(nc, Scope(nc, ctx, "b", top), ident, qkh, qkl, vd, aod)
        with ExitStack() as ctx:
            phase_proj(nc, Scope(nc, ctx, "c", top), ident, adaT, eps, gd, xf, aod, W_proj, b_proj, b_fc2, hth, htl, y1)
        with ExitStack() as ctx:
            phase_mlp(nc, Scope(nc, ctx, "d", top), gd, hth, htl, y1, y2, of, W_fc1, b_fc1, W_fc2)


def phase_setup(nc, P, ident, adaT, eps, bq, gd, wh, wl, wm, wr, cond, W_ada, b_ada, W_qkv, b_qkv):
    NA = 6 * C // 8
    with ExitStack() as ctx:
        S = Scope(nc, ctx, "s", P.sems)
        q = Queues()
        wa = S.sb("wa", [128, KT, 6 * C])
        cT = S.sb("cT", [128, KT, 2])
        ex = S.sb("ex", [128, KT, 2])
        e1 = S.sb("e1", [128, KT, 2])
        rc = S.sb("rc", [128, KT, 2])
        sc = S.sb("sc", [128, KT, 2])
        bad = S.sb("bad", [2, 6 * C])
        row = S.sb("row", [2, 6, 640])
        stg = [S.sb(f"stg{i}", [128, 3 * C]) for i in range(2)]
        ps = S.ps("ps", [128, 8, 512])
        s_c, s_b, s_bq, s_g = S.sem("c"), S.sem("b"), S.sem("bq"), S.sem("g")
        s_id, s_z, s_zz = S.sem("id"), S.sem("z"), S.sem("zz")
        s_wa = [S.sem(f"wa{k}") for k in range(KT)]
        s_si, s_mm, s_row, s_tr, s_ad = S.sem("si"), S.sem("mm"), S.sem("row"), S.sem("tr"), S.sem("ad")
        s_ld = [S.sem(f"ld{i}") for i in range(2)]
        s_hi, s_lo = S.sem("hi"), S.sem("lo")

        q.put("gpsimd", lambda e: e.memset(ident[:, :], 0.0), (), s_id)
        tid = q.put("gpsimd", lambda e: e.affine_select(
            out=ident[:, :], in_=ident[:, :], compare_op=ALU.not_equal, fill=1.0, base=0, pattern=[[-1, 128]],
            channel_multiplier=1), (s_id.now(),), s_id)
        zc = q.put("vector", lambda e: e.memset(cT[:, :, :], 0.0), (), s_z)
        q.put("vector", lambda e: e.memset(eps[:, :], EPS), (), s_zz)
        for b in range(2):
            q.put("sync", lambda e, b=b: e.dma_start(cT[:, 0:4, b], cond[b, 0:512].rearrange("(k p) -> p k", p=128),
                                                  allow_slow_non_contiguous=True),
                  (zc,), s_c, 16)
            tc = q.put("sync", lambda e, b=b: e.dma_start(cT[0:64, 4, b:b + 1],
                                                         cond[b, 512:576].rearrange("(p o) -> p o", o=1),
                                                         allow_slow_non_contiguous=True),
                       (zc,), s_c, 16)
        for kt in range(KT):
            n = 128 if kt < 4 else 64
            q.put("sync", lambda e, kt=kt, n=n: e.dma_start(wa[0:n, kt, :], W_ada[kt * 128:kt * 128 + n, :]), (),
                  s_wa[kt], 16)
        for b in range(2):
            tb = q.put("sync", lambda e, b=b: e.dma_start(bad[b:b + 1, :], b_ada.rearrange("(o n) -> o n", o=1)), (),
                       s_b, 16)
        q.put("sync", lambda e: e.dma_start(bq[:, :], b_qkv[0:2 * C].rearrange("(f p) -> p f", p=128),
                                            allow_slow_non_contiguous=True), (), s_bq, 16)

        t = q.put("scalar", lambda e: e.activation(ex[:, :, :], cT[:, :, :], ACT.Exp, scale=-1.0), (tc,), s_si)
        t = q.put("vector", lambda e: e.tensor_scalar(e1[:, :, :], ex[:, :, :], 1.0, None, ALU.add), (t,), s_si)
        t = q.put("vector", lambda e: e.reciprocal(rc[:, :, :], e1[:, :, :]), (t,), s_si)
        t = q.put("vector", lambda e: e.tensor_tensor(sc[:, :, :], cT[:, :, :], rc[:, :, :], ALU.mult), (t, tc), s_si)
        for kt in range(KT):
            n = 128 if kt < 4 else 64
            for j in range(8):
                tm = q.put("tensor", lambda e, kt=kt, n=n, j=j: e.matmul(
                    ps[0:2, j, 0:NA], sc[0:n, kt, :], wa[0:n, kt, j * NA:(j + 1) * NA], start=kt == 0,
                    stop=kt == KT - 1), (t, (s_wa[kt], 16)), s_mm)
        tr = None
        for v in range(6):
            for a, b_ in ((0, C),):
                lo_, hi_ = v * C, v * C + C
                while lo_ < hi_:
                    j = lo_ // NA
                    m = min(hi_, (j + 1) * NA)
                    tr = q.put("vector", lambda e, v=v, lo_=lo_, m=m, j=j: e.tensor_tensor(
                        row[:, v, lo_ - v * C:m - v * C], ps[0:2, j, lo_ - j * NA:m - j * NA], bad[:, lo_:m], ALU.add),
                        (tm, tb), s_row)
                    lo_ = m
            tr = q.put("vector", lambda e, v=v: e.tensor_copy(row[:, v, C:640], row[:, v, 512:C]), (tr,), s_row)
        for g, v in enumerate((2, 5)):
            tg = q.put("sync", lambda e, g=g, v=v: e.dma_start(gd[g, :, :], row[:, v, 0:C]), (tr,), s_g, 16)
        for v in range(6):
            for kt in range(KT):
                tt = q.put("tensor", lambda e, v=v, kt=kt: e.transpose(
                    ps[:, 0, (v * KT + kt) * 2:(v * KT + kt) * 2 + 2], row[:, v, kt * 128:kt * 128 + 128],
                    ident[0:2, 0:2]), (tr, tid), s_tr)
        ta = q.put("vector", lambda e: e.tensor_copy(adaT[:, :, :, :].rearrange("p v k b -> p (v k b)"),
                                                     ps[:, 0, 0:60]), (tt,), s_ad)
        for v in (1, 4):
            q.put("vector", lambda e, v=v: e.tensor_scalar(adaT[:, v, :, :], adaT[:, v, :, :], 1.0, None, ALU.add),
                  (ta,), s_ad)
        split_rows(q, S, W_qkv, wh, wl, wm, wr, 0, 3 * C, stg, s_ld, s_hi, s_lo, s_zz, [None, None])
        drain(q, [s_c, s_b, s_bq, s_g] + s_ld)
        q.emit(nc)


def phase_qkv(nc, A, ident, adaT, eps, bq, wh, wl, wm, wr, xf, b_qkv, qkh, qkl, vd):
    q = Queues()
    xin = [A.sb(f"x{i}", [128, 4, C]) for i in range(2)]
    xn = A.sb("xn", [128, 4, 640])
    st = A.sb("st", [128, 4, 2, 6])
    mv = A.sb("mv", [128, 4, 2])
    sd = A.sb("sd", [128, 4])
    rs = A.sb("rs", [128, 4])
    hf = [A.sb(f"hf{i}", [128, CH]) for i in range(2)]
    hh = [A.sb(f"hh{i}", [128, KT, CH], R) for i in range(2)]
    lo = [A.sb(f"lo{i}", [128, 4, CH], R) for i in range(2)]
    tf = [A.sb(f"tf{i}", [128, CH]) for i in range(2)]
    th = [A.sb(f"th{i}", [128, CH], R) for i in range(2)]
    tl = [A.sb(f"tl{i}", [128, CH], R) for i in range(2)]
    vc = [A.sb(f"vc{i}", [128, 4, H, D + 1]) for i in range(2)]
    bv = A.sb("bv", [128, C])
    pt = [A.ps(f"pt{i}", [128, 512]) for i in range(2)]
    pm = [A.ps(f"pm{i}", [128, 512]) for i in range(4)]
    s_x = [A.sem(f"x{i}") for i in range(2)]
    s_bv, s_st, s_sd, s_rs, s_xn = A.sem("bv"), A.sem("st"), A.sem("sd"), A.sem("rs"), A.sem("xn")
    s_tp, s_hf, s_hh, s_lo = A.sem("tp"), A.sem("hf"), A.sem("hh"), A.sem("lo")
    s_mm, s_tf, s_tl, s_vc, s_on = A.sem("mm"), A.sem("tf"), A.sem("tl"), A.sem("vc"), A.sem("on")
    s_qo = [A.sem(f"qo{i}") for i in range(2)]
    s_vo = [A.sem(f"vo{i}") for i in range(2)]

    tbv = q.put("sync", lambda e: e.dma_start(bv[:, :], b_qkv[2 * C:3 * C].partition_broadcast(128)), (), s_bv, 16)
    for i in range(2):
        ton = q.put("vector", lambda e, i=i: e.memset(vc[i][:, :, :, D:D + 1].rearrange("p t h o -> p (t h) o"), 1.0),
                    (), s_on)
    free = {"x": [None, None], "xn": None, "pt": [None, None], "hf": [None, None], "h": [None, None],
            "pm": [None] * 4, "tf": [None, None], "tl": [None, None], "vc": [None, None], "rs": None}
    ready = {}
    n_pt = [0]
    n_pm = [0]

    def load(c):
        i = c % 2
        return q.put("sync", lambda e: e.dma_start(
            xin[i][:, :, :], xf[c * CH:(c + 1) * CH, :].rearrange("(t p) c -> p t c", p=128)), (free["x"][i],),
            s_x[i], 16)

    def prepare(c):
        i, b = c % 2, c // (NCH // 2)
        tx = load(c)
        yield
        for t in range(4):
            for g in range(2):
                ts = q.put("vector", lambda e, t=t, g=g: e.bn_stats(
                    st[:, t, g, :], xin[i][:, t, g * HALF:(g + 1) * HALF]), (tx, free["rs"]), s_st)
            ts = q.put("vector", lambda e, t=t: e.bn_aggr(mv[:, t, :], st[:, t, :, :]), (ts, free["xn"]), s_st)
        tsd = q.put("scalar", lambda e: e.activation(sd[:, :], mv[:, :, 1], ACT.Sqrt, bias=eps[:, 0:1]), (ts,), s_sd)
        trs = q.put("vector", lambda e: e.reciprocal(rs[:, :], sd[:, :]), (tsd,), s_rs)
        free["rs"] = trs
        yield
        for t in range(4):
            for a, z, d in ((0, C, 0), (512, C, C)):
                txn = q.put("vector", lambda e, t=t, a=a, z=z, d=d: e.tensor_scalar(
                    xn[:, t, d:d + z - a], xin[i][:, t, a:z], mv[:, t, 0:1], rs[:, t:t + 1], ALU.subtract, ALU.mult),
                    (trs, free["xn"]), s_xn)
            if t == 1:
                yield
        free["x"][i] = txn
        yield
        for kt in range(KT):
            j = n_pt[0] % 2
            n_pt[0] += 1
            for t in range(4):
                ttp = q.put("tensor", lambda e, t=t, kt=kt, j=j: e.transpose(
                    pt[j][:, t * 128:t * 128 + 128], xn[:, t, kt * 128:kt * 128 + 128], ident[:, :]),
                    (txn, free["pt"][j]), s_tp)
            thf = q.put("scalar", lambda e, kt=kt, j=j: e.activation(
                hf[j][:, :], pt[j][:, :], ACT.Identity, bias=adaT[:, 0, kt, b:b + 1], scale=adaT[:, 1, kt, b:b + 1]),
                (ttp, free["hf"][j]), s_hf)
            free["pt"][j] = thf
            thh = q.put("vector", lambda e, kt=kt, j=j: e.tensor_copy(hh[i][:, kt, :], hf[j][:, :]),
                        (thf, free["h"][i]), s_hh)
            if kt < 4:
                tlo = q.put("vector", lambda e, kt=kt, j=j: e.tensor_tensor(
                    lo[i][:, kt, :], hf[j][:, :], hh[i][:, kt, :].bitcast(F), ALU.subtract), (thh, free["h"][i]), s_lo)
            else:
                tlo = q.put("vector", lambda e, kt=kt, j=j: e.tensor_tensor(
                    hh[i][64:128, kt, :], hf[j][64:128, :], hh[i][64:128, kt, :].bitcast(F), ALU.subtract),
                    (thh,), s_lo)
            free["hf"][j] = tlo
            yield
        free["xn"] = ttp
        ready[c] = [thh, tlo]

    for _ in prepare(0):
        pass
    for c in range(NCH):
        i = c % 2
        nxt = prepare(c + 1) if c + 1 < NCH else iter(())
        for f in range(NF):
            m, j = n_pm[0] % 4, f % 2
            n_pm[0] += 1
            ps_ = passes(wh, wl, wm, wr, hh[i], lo[i], slice(f * 128, f * 128 + 128), slice(0, CH))
            for n, (w, a) in enumerate(ps_):
                tm = q.put("tensor", lambda e, w=w, a=a, n=n, m=m: e.matmul(
                    pm[m][:, :], w, a, start=n == 0, stop=n == 13),
                    ready[c] + [free["pm"][m]], s_mm if n == 13 else None)
            tt = q.put("scalar", lambda e, f=f, j=j, m=m: e.activation(
                tf[j][:, :], pm[m][:, :], ACT.Identity, bias=bq[:, f:f + 1]), (tm, free["tf"][j]), s_tf)
            tt = q.put("scalar", lambda e, f=f, j=j, m=m: e.activation(
                th[j][:, :], pm[m][:, :], ACT.Identity, bias=bq[:, f:f + 1]), (tm, free["tl"][j]), s_tf)
            free["pm"][m] = tt
            tlw = q.put("vector", lambda e, j=j: e.tensor_tensor(
                tl[j][:, :], tf[j][:, :], th[j][:, :].bitcast(F), ALU.subtract), (tt, free["tl"][j]), s_tl)
            free["tf"][j] = tlw
            q.put("sync", lambda e, f=f, j=j, c=c: e.dma_start(
                qkh[f * 128:f * 128 + 128, c * CH:(c + 1) * CH], th[j][:, :].bitcast(F)), (tt,), s_qo[j], 16)
            free["tl"][j] = q.put("sync", lambda e, f=f, j=j, c=c: e.dma_start(
                qkl[f * 128:f * 128 + 128, c * CH:(c + 1) * CH], tl[j][:, :].bitcast(F)), (tlw,), s_qo[j], 16)
            next(nxt, None)
        for t in range(4):
            for n2 in range(2):
                m = n_pm[0] % 4
                n_pm[0] += 1
                ps_ = passes_t(wh, wl, wm, wr, hh[i], lo[i], slice(2 * C + n2 * HALF, 2 * C + (n2 + 1) * HALF),
                               slice(t * 128, t * 128 + 128))
                for n, (w, a) in enumerate(ps_):
                    tm = q.put("tensor", lambda e, w=w, a=a, n=n, m=m: e.matmul(
                        pm[m][:, 0:HALF], w, a, start=n == 0, stop=n == 13),
                        ready[c] + [free["pm"][m]], s_mm if n == 13 else None)
                tv = q.put("vector", lambda e, t=t, n2=n2, m=m, i=i: e.tensor_tensor(
                    vc[i][:, t, n2 * 8:n2 * 8 + 8, 0:D], pm[m][:, 0:HALF].rearrange("p (h d) -> p h d", d=D),
                    bv[:, n2 * HALF:(n2 + 1) * HALF].rearrange("p (h d) -> p h d", d=D), ALU.add),
                    (tm, tbv, ton, free["vc"][i]), s_vc)
                free["pm"][m] = tv
            next(nxt, None)
        free["h"][i] = tm
        free["vc"][i] = q.put("sync", lambda e, i=i, c=c: e.dma_start(
            vd[c * CH:(c + 1) * CH, :].rearrange("(t p) n -> p t n", p=128),
            vc[i][:, :, :, :].rearrange("p t h d -> p t (h d)")), (tv, ton), s_vo[i], 16)
        for _ in nxt:
            pass
    drain(q, s_qo + s_vo + s_x + [s_bv])
    q.emit(nc)


def phase_attention(nc, A, ident, qkh, qkl, vd, aod):
    q = Queues()
    NB = 3
    NH = B * H
    qs = [A.sb(f"qs{i}", [128, L], R) for i in range(NB)]
    ks = [A.sb(f"ks{i}", [128, L], R) for i in range(NB)]
    vf = [A.sb(f"vf{i}", [128, 16, VW]) for i in range(2)]
    vs = [A.sb(f"vs{i}", [128, 16, VW], R) for i in range(2)]
    NP = 5
    pt = [A.sb(f"pt{i}", [128, 1024]) for i in range(NP)]
    ph = [A.sb(f"ph{i}", [128, 1024], R) for i in range(3)]
    pl = [A.sb(f"pl{i}", [128, 1024], R) for i in range(3)]
    oa = A.sb("oa", [D + 1, 1024])
    ob = A.sb("ob", [D + 1, 1024])
    oc = A.sb("oc", [D + 1, 1024])
    rc = A.sb("rc", [128, 8])
    ao = [A.sb(f"ao{i}", [128, 8, D]) for i in range(2)]
    mx = A.sb("mx", [128, 16, 4])
    nm = A.sb("nm", [128, 16])
    mh = A.sb("mh", [16, 128], R)
    ml = A.sb("ml", [16, 128], R)
    st = [A.ps(f"st{i}", [128, 1024]) for i in range(2)]
    op = A.ps("op", [128, 1024])
    sp = [A.ps(f"sp{i}", [128, 512]) for i in range(2)]
    s_qk = [A.sem(f"qk{i}") for i in range(NB)]
    s_v = [A.sem(f"v{i}") for i in range(2)]
    s_m = [A.sem(f"m{i}") for i in range(NB)]
    s_ao = [A.sem(f"ao{i}") for i in range(2)]
    s_ini, s_vs, s_s, s_mx, s_nm, s_mt, s_mh = (A.sem("ini"), A.sem("vs"), A.sem("s"), A.sem("mx"), A.sem("nm"),
                                                A.sem("mt"), A.sem("mh"))
    s_st, s_p, s_ph, s_pl, s_pv = A.sem("st"), A.sem("p"), A.sem("ph"), A.sem("pl"), A.sem("pv")
    s_oe, s_oc, s_ot, s_rc, s_an = A.sem("oe"), A.sem("oc"), A.sem("ot"), A.sem("rc"), A.sem("an")

    for i in range(NB):
        q.put("vector", lambda e, i=i: e.memset(ks[i][96:128, :].bitcast(F), 1.0), (), s_ini)
    for i in range(2):
        q.put("vector", lambda e, i=i: e.memset(vf[i][:, :, :], 0.0), (), s_ini)
        q.put("vector", lambda e, i=i: e.memset(vs[i][:, :, :].bitcast(F), 0.0), (), s_ini)
    ini = s_ini.now()

    free = {"qk": [None] * NB, "v": [None, None], "vs": [None, None], "st": [None, None], "pt": [None] * NP,
            "ph": [None] * 3, "pl": [None] * 3, "sp": [None, None], "op": None, "mx": None, "nm": None, "mh": None,
            "oa": None, "oc": None, "rc": None, "ao": [None, None]}
    tqk, tv, tvs, tm_ = {}, {}, {}, {}
    n_sp, n_ph = [0], [0]

    def load(h):
        i, b, hd = h % NB, h // H, h % H
        sl = slice(b * L, (b + 1) * L)
        for dst, src, r in ((qs, qkh, 0), (qs, qkl, 36), (qs, qkh, 72), (ks, qkh, 0), (ks, qkh, 36), (ks, qkl, 72)):
            f0 = hd * D + (C if dst is ks else 0)
            tqk[h] = q.put("sync", lambda e, dst=dst, src=src, r=r, f0=f0: e.dma_start(
                dst[i][r:r + D, :].bitcast(F), src[f0:f0 + D, sl]), (ini, free["qk"][i]), s_qk[i], 16)

    def load_v(h):
        b, hd, v = h // H, h % H, h % 2
        sl = slice(b * L, (b + 1) * L)
        tv[h] = q.put("sync", lambda e: e.dma_start(
            vf[v][:, :, 0:D + 1],
            vd[sl, hd * (D + 1):(hd + 1) * (D + 1)].rearrange("(k p) d -> p k d", p=128)), (ini, free["v"][v]),
            s_v[v], 16)

    def split_v(h):
        v = h % 2
        t = q.put("vector", lambda e: e.tensor_copy(vs[v][:, :, 0:D + 1], vf[v][:, :, 0:D + 1]),
                  (ini, tv[h], free["v"][v]), s_vs)
        tvs[h] = q.put("vector", lambda e: e.tensor_tensor(
            vs[v][:, :, 64:VW], vf[v][:, :, 0:D + 1], vs[v][:, :, 0:D + 1].bitcast(F), ALU.subtract), (t,), s_vs)

    def slot():
        j = n_sp[0] % 2
        n_sp[0] += 1
        return j

    def score_max(h, n):
        qb, k4 = n // 4, n % 4
        i, j = h % NB, slot()
        t = q.put("tensor", lambda e: e.matmul(
            sp[j][:, :], qs[i][0:108, qb * 128:qb * 128 + 128], ks[i][0:108, k4 * 512:k4 * 512 + 512], start=True,
            stop=True), (tqk[h], free["sp"][j]), s_s)
        free["sp"][j] = q.put("vector", lambda e: e.tensor_reduce(mx[:, qb, k4:k4 + 1], sp[j][:, :], AX.X, ALU.max),
                              (t, free["mx"]), s_mx)

    def max_rows(h):
        i, j = h % NB, slot()
        t = q.put("vector", lambda e: e.tensor_reduce(nm[:, :], mx[:, :, :], AX.X, ALU.max, negate=True),
                  (s_mx.now(), free["nm"]), s_nm)
        free["mx"] = t
        t = q.put("tensor", lambda e: e.transpose(sp[j][0:16, 0:128], nm[:, :], ident[:, :]), (t, free["sp"][j]), s_mt)
        free["nm"] = t
        t1 = q.put("vector", lambda e: e.tensor_copy(mh[:, :], sp[j][0:16, 0:128]), (t, free["mh"]), s_mh)
        t2 = q.put("vector", lambda e: e.tensor_tensor(ml[:, :], sp[j][0:16, 0:128], mh[:, :].bitcast(F),
                                                       ALU.subtract), (t1, free["mh"]), s_mh)
        free["sp"][j] = t2
        q.put("sync", lambda e: e.dma_start(qs[i][108:109, :].bitcast(F), mh[:, :].bitcast(F)),
              (t1,), s_m[i], 16)
        tm_[h] = q.put("sync", lambda e: e.dma_start(qs[i][109:110, :].bitcast(F), ml[:, :].bitcast(F)), (t2,),
                       s_m[i], 16)
        free["mh"] = tm_[h]

    pend = {}

    def scores_t(g):
        h, u, kb = g // 32, (g // 16) % 2, g % 16
        i, j = h % NB, g % 2
        for a in range(2):
            t = q.put("tensor", lambda e, a=a: e.matmul(
                st[j][:, a * 512:a * 512 + 512], ks[i][0:110, kb * 128:kb * 128 + 128],
                qs[i][0:110, u * 1024 + a * 512:u * 1024 + a * 512 + 512], start=True, stop=True),
                (ini, tqk[h], tm_[h], free["st"][j]), s_st if a else None)
        return t

    def soft(g, t):
        j, p, kb = g % 2, g % NP, g % 16
        tp = q.put("scalar", lambda e: e.activation(pt[p][:, :], st[j][:, :], ACT.Exp, scale=SCALE),
                   (t, free["pt"][p]), s_p)
        free["st"][j] = tp
        if kb in SPLIT:
            r = n_ph[0] % 3
            n_ph[0] += 1
            th = q.put("scalar", lambda e: e.activation(ph[r][:, :], pt[p][:, :], ACT.Copy), (tp, free["ph"][r]), s_ph)
            tl = q.put("vector", lambda e: e.tensor_tensor(pl[r][:, :], pt[p][:, :], ph[r][:, :].bitcast(F),
                                                           ALU.subtract), (th, free["ph"][r]), s_pl)
            free["pt"][p] = tl
            pend[g] = (r, th, tl)
        else:
            pend[g] = (None, tp, tp)

    def pv(g):
        h, u, kb = g // 32, (g // 16) % 2, g % 16
        v, p = h % 2, g % NP
        r, t0, t1 = pend.pop(g)
        first, last = kb == 0, kb == 15
        if r is None:
            parts = [(vf[v][:, kb, :], pt[p], t0)]
        else:
            parts = [(vs[v][:, kb, :], ph[r], t0), (vs[v][:, kb, :], pl[r], t1)]
        for n, (w, m, tk) in enumerate(parts):
            for a in range(2):
                t = q.put("tensor", lambda e, w=w, m=m, a=a, n=n: e.matmul(
                    op[0:VW, a * 512:a * 512 + 512], w, m[:, a * 512:a * 512 + 512],
                    start=first and n == 0, stop=last and n == len(parts) - 1),
                    (tk, tvs[h], free["op"] if first else None), s_pv)
        if r is None:
            free["pt"][p] = t
        else:
            free["ph"][r] = t
        if last:
            if u == 1:
                free["v"][v] = t
            return t
        return None

    def o_out(g, t):
        free["op_src"] = t
        q.put("scalar", lambda e: e.activation(oa[:, :], op[64:VW, :], ACT.Copy), (t, free["oa"]), s_oe)
        t = q.put("scalar", lambda e: e.activation(ob[:, :], op[0:D + 1, :], ACT.Copy), (t, free["oa"]), s_oe)
        free["op"] = t
        t = q.put("gpsimd", lambda e: e.tensor_tensor(oc[:, :], oa[:, :], ob[:, :], ALU.add), (t, free["oc"]), s_oc)
        free["oa"] = t
        return t

    def o_norm(g, t):
        h, u = g // 32, (g // 16) % 2
        b, hd = h // H, h % H
        j, k = slot(), (g // 16) % 2
        for n in range(8):
            tt = q.put("tensor", lambda e, n=n: e.transpose(sp[j][:, n * 37:n * 37 + 37], oc[:, n * 128:n * 128 + 128],
                                                            ident[0:37, 0:37]), (t, free["sp"][j]), s_ot)
        free["oc"] = tt
        view = sp[j][:, 0:296].rearrange("p (n d) -> p n d", d=37)
        t1 = q.put("vector", lambda e: e.reciprocal(rc[:, :], view[:, :, D]), (tt, free["rc"]), s_rc)
        t2 = q.put("vector", lambda e: e.tensor_tensor(
            ao[k][:, :, :], view[:, :, 0:D], rc[:, :].unsqueeze(2).to_broadcast([128, 8, D]), ALU.mult),
            (t1, free["ao"][k]), s_an)
        free["sp"][j] = t2
        free["rc"] = t2
        r0 = b * L + u * 1024
        free["ao"][k] = q.put("sync", lambda e: e.dma_start(
            aod[r0:r0 + 1024, hd * D:(hd + 1) * D].rearrange("(n p) d -> p n d", p=128), ao[k][:, :, :]), (t2,),
            s_ao[k], 16)

    load(0)
    load(1)
    load_v(0)
    split_v(0)
    for n in range(64):
        score_max(0, n)
    max_rows(0)
    LAG = 2
    G = NH * 32
    done, norm = None, None
    for g in range(G + LAG + 4):
        h, s = g // 32, g % 32
        if g < G:
            if s == 0 and h + 2 < NH:
                load(h + 2)
            t = scores_t(g)
            if g >= LAG:
                tl = pv(g - LAG)
                if tl is not None:
                    done = (g - LAG, tl)
                    done = (g - LAG, o_out(*done))
                    norm = (g + 2, done)
            soft(g, t)
            if s == 31:
                free["qk"][h % NB] = s_st.now()
            if h + 1 < NH:
                if s == 3:
                    load_v(h + 1)
                if s == 16:
                    split_v(h + 1)
                for n in range(s * 64 // 26, min(64, (s + 1) * 64 // 26)):
                    score_max(h + 1, n)
                if s == 26:
                    max_rows(h + 1)
        elif g - LAG < G:
            tl = pv(g - LAG)
            if tl is not None:
                norm = (g + 2, (g - LAG, o_out(g - LAG, tl)))
        if norm is not None and norm[0] == g:
            o_norm(*norm[1])
            norm = None
    drain(q, s_ao + s_m + s_qk + s_v)
    q.emit(nc)


def phase_proj(nc, A, ident, adaT, eps, gd, xf, aod, W_proj, b_proj, b_fc2, hth, htl, y1):
    q = Queues()
    wh = A.sb("wh", [128, 4, C], R)
    wl = A.sb("wl", [128, 4, C], R)
    wm = A.sb("wm", [128, C], R)
    wr = A.sb("wr", [128, C], R)
    stg = [A.sb(f"stg{i}", [128, C]) for i in range(2)]
    gt = A.sb("gt", [128, 2, 2, C])
    bb = A.sb("bb", [128, 2, C])
    gb = A.sb("gb", [128, 2, 2, C])
    ai = [A.sb(f"ai{i}", [128, 4, 640]) for i in range(2)]
    xi = [A.sb(f"xi{i}", [128, 4, C]) for i in range(2)]
    x1 = [A.sb(f"x1{i}", [128, 4, C]) for i in range(2)]
    xo = A.sb("xo", [128, 4, C])
    ug = [A.sb(f"ug{i}", [128, HALF]) for i in range(2)]
    xn = A.sb("xn", [128, 4, 640])
    st = A.sb("st", [128, 4, 2, 6])
    mv = A.sb("mv", [128, 4, 2])
    sd = A.sb("sd", [128, 4])
    rs = A.sb("rs", [128, 4])
    ah = A.sb("ah", [128, KT, CH], R)
    al = A.sb("al", [128, 4, CH], R)
    hf = [A.sb(f"hf{i}", [128, CH]) for i in range(2)]
    hh = A.sb("hh", [128, KT, CH], R)
    hl = A.sb("hl", [128, 4, CH], R)
    pt = [A.ps(f"pt{i}", [128, 512]) for i in range(4)]
    pm = [A.ps(f"pm{i}", [128, 512]) for i in range(4)]
    s_w = [A.sem(f"w{i}") for i in range(2)]
    s_whi, s_wlo, s_z, s_bc, s_gb = A.sem("whi"), A.sem("wlo"), A.sem("z"), A.sem("bc"), A.sem("gb")
    s_a = [A.sem(f"a{i}") for i in range(2)]
    s_x = [A.sem(f"x{i}") for i in range(2)]
    s_tp, s_ah, s_al, s_mm, s_ug, s_xg, s_x1 = (A.sem("tp"), A.sem("ah"), A.sem("al"), A.sem("mm"), A.sem("ug"),
                                                A.sem("xg"), A.sem("xa"))
    s_st, s_sd, s_rs, s_xn, s_xo, s_hf, s_hh, s_hl = (A.sem("st"), A.sem("sd"), A.sem("rs"), A.sem("xn"), A.sem("xo"),
                                                      A.sem("hf"), A.sem("hh"), A.sem("hl"))
    s_y, s_ho = A.sem("y"), A.sem("ho")

    tw = split_rows(q, A, W_proj, wh, wl, wm, wr, 0, C, stg, s_w, s_whi, s_wlo, s_z, [None, None])
    for g in range(2):
        for b in range(2):
            q.put("sync", lambda e, g=g, b=b: e.dma_start(gt[:, g, b, :], gd[g, b, :].partition_broadcast(128)), (),
                  s_bc, 16)
    for g, src in enumerate((b_proj, b_fc2)):
        tbc = q.put("sync", lambda e, g=g, src=src: e.dma_start(bb[:, g, :], src.partition_broadcast(128)), (),
                    s_bc, 16)
    for g in range(2):
        for b in range(2):
            tgb = q.put("gpsimd", lambda e, g=g, b=b: e.tensor_tensor(gb[:, g, b, :], gt[:, g, b, :], bb[:, g, :],
                                                                      ALU.mult), (tbc,), s_gb)
    free = {"ai": [None, None], "xi": [None, None], "pt": [None] * 4, "pm": [None] * 4, "ah": None, "ug": [None, None],
            "x1": [None, None], "xo": None, "xn": None, "rs": None, "hf": [None, None], "hh": None}
    n_pt, n_pm, n_ug = [0], [0], [0]
    tx1 = {}

    def first(c):
        i, b = c % 2, c // (NCH // 2)
        rows = slice(c * CH, (c + 1) * CH)
        q.put("sync", lambda e: e.dma_start(ai[i][:, :, 0:C], aod[rows, :].rearrange("(t p) c -> p t c", p=128)),
              (free["ai"][i],), s_a[i], 16)
        ta = q.put("sync", lambda e: e.dma_start(
            ai[i][:, :, C:640], aod[rows, 512:C].rearrange("(t p) c -> p t c", p=128)), (free["ai"][i],), s_a[i], 16)
        tx = q.put("sync", lambda e: e.dma_start(xi[i][:, :, :], xf[rows, :].rearrange("(t p) c -> p t c", p=128)),
                   (free["xi"][i],), s_x[i], 16)
        for t in range(4):
            txg = q.put("gpsimd", lambda e, t=t: e.tensor_tensor(xi[i][:, t, :], xi[i][:, t, :], gb[:, 0, b, :],
                                                                 ALU.add), (tx, tgb), s_xg)
        for kt in range(KT):
            j = n_pt[0] % 4
            n_pt[0] += 1
            for t in range(4):
                ttp = q.put("tensor", lambda e, t=t, kt=kt, j=j: e.transpose(
                    pt[j][:, t * 128:t * 128 + 128], ai[i][:, t, kt * 128:kt * 128 + 128], ident[:, :]),
                    (ta, free["pt"][j]), s_tp)
            tah = q.put("scalar", lambda e, kt=kt, j=j: e.activation(ah[:, kt, :], pt[j][:, :], ACT.Copy),
                        (ttp, free["ah"]), s_ah)
            if kt < 4:
                tal = q.put("vector", lambda e, kt=kt, j=j: e.tensor_tensor(
                    al[:, kt, :], pt[j][:, :], ah[:, kt, :].bitcast(F), ALU.subtract), (tah, free["ah"]), s_al)
            else:
                tal = q.put("vector", lambda e, kt=kt, j=j: e.tensor_tensor(
                    ah[64:128, kt, :], pt[j][64:128, :], ah[64:128, kt, :].bitcast(F), ALU.subtract), (tah,), s_al)
            free["pt"][j] = tal
        free["ai"][i] = ttp
        for t in range(4):
            for n2 in range(2):
                m, k = n_pm[0] % 4, n_ug[0] % 2
                n_pm[0] += 1
                n_ug[0] += 1
                cs = slice(n2 * HALF, (n2 + 1) * HALF)
                for n, (w, a) in enumerate(passes_t(wh, wl, wm, wr, ah, al, cs, slice(t * 128, t * 128 + 128))):
                    tm = q.put("tensor", lambda e, w=w, a=a, n=n, m=m: e.matmul(
                        pm[m][:, 0:HALF], w, a, start=n == 0, stop=n == 13),
                        tw + [tah, tal, free["pm"][m]], s_mm if n == 13 else None)
                tu = q.put("vector", lambda e, m=m, k=k, cs=cs: e.tensor_tensor(
                    ug[k][:, :], pm[m][:, 0:HALF], gt[:, 0, b, cs], ALU.mult), (tm, tbc, free["ug"][k]), s_ug)
                free["pm"][m] = tu
                t1 = q.put("vector", lambda e, t=t, k=k, cs=cs: e.tensor_tensor(
                    x1[i][:, t, cs], ug[k][:, :], xi[i][:, t, cs], ALU.add), (tu, txg, free["x1"][i]), s_x1)
                free["ug"][k] = t1
        free["ah"] = tm
        free["xi"][i] = t1
        tx1[c] = t1

    def second(c):
        i, b = c % 2, c // (NCH // 2)
        rows = slice(c * CH, (c + 1) * CH)
        for t in range(4):
            for g in range(2):
                ts = q.put("vector", lambda e, t=t, g=g: e.bn_stats(
                    st[:, t, g, :], x1[i][:, t, g * HALF:(g + 1) * HALF]), (tx1[c], free["rs"]), s_st)
            ts = q.put("vector", lambda e, t=t: e.bn_aggr(mv[:, t, :], st[:, t, :, :]), (ts, free["xn"]), s_st)
        tsd = q.put("scalar", lambda e: e.activation(sd[:, :], mv[:, :, 1], ACT.Sqrt, bias=eps[:, 0:1]), (ts,), s_sd)
        trs = q.put("vector", lambda e: e.reciprocal(rs[:, :], sd[:, :]), (tsd,), s_rs)
        free["rs"] = trs
        for t in range(4):
            for a, z, d in ((0, C, 0), (512, C, C)):
                txn = q.put("vector", lambda e, t=t, a=a, z=z, d=d: e.tensor_scalar(
                    xn[:, t, d:d + z - a], x1[i][:, t, a:z], mv[:, t, 0:1], rs[:, t:t + 1], ALU.subtract, ALU.mult),
                    (trs, free["xn"]), s_xn)
            txo = q.put("gpsimd", lambda e, t=t: e.tensor_tensor(xo[:, t, :], x1[i][:, t, :], gb[:, 1, b, :], ALU.add),
                        (tx1[c], tgb, free["xo"]), s_xo)
        free["x1"][i] = txn
        free["xo"] = q.put("sync", lambda e: e.dma_start(y1[rows, :].rearrange("(t p) c -> p t c", p=128),
                                                         xo[:, :, :]), (txo,), s_y, 16)
        for kt in range(KT):
            j, k = n_pt[0] % 4, kt % 2
            n_pt[0] += 1
            for t in range(4):
                ttp = q.put("tensor", lambda e, t=t, kt=kt, j=j: e.transpose(
                    pt[j][:, t * 128:t * 128 + 128], xn[:, t, kt * 128:kt * 128 + 128], ident[:, :]),
                    (txn, free["pt"][j]), s_tp)
            thf = q.put("scalar", lambda e, kt=kt, j=j, k=k: e.activation(
                hf[k][:, :], pt[j][:, :], ACT.Identity, bias=adaT[:, 3, kt, b:b + 1], scale=adaT[:, 4, kt, b:b + 1]),
                (ttp, free["hf"][k]), s_hf)
            free["pt"][j] = thf
            thh = q.put("vector", lambda e, kt=kt, k=k: e.tensor_copy(hh[:, kt, :], hf[k][:, :]), (thf, free["hh"]),
                        s_hh)
            if kt < 4:
                thl = q.put("vector", lambda e, kt=kt, k=k: e.tensor_tensor(
                    hl[:, kt, :], hf[k][:, :], hh[:, kt, :].bitcast(F), ALU.subtract), (thh, free["hh"]), s_hl)
            else:
                thl = q.put("vector", lambda e, kt=kt, k=k: e.tensor_tensor(
                    hh[64:128, kt, :], hf[k][64:128, :], hh[64:128, kt, :].bitcast(F), ALU.subtract), (thh,), s_hl)
            free["hf"][k] = thl
        free["xn"] = ttp
        q.put("sync", lambda e: e.dma_start(hth[:, :, rows].rearrange("k p t -> p k t"), hh[:, :, :].bitcast(F)),
              (thh, thl), s_ho, 16)
        free["hh"] = q.put("sync", lambda e: e.dma_start(htl[:, :, rows].rearrange("k p t -> p k t"),
                                                         hl[:, :, :].bitcast(F)), (thl,), s_ho, 16)

    for c in range(NCH + 1):
        if c < NCH:
            first(c)
        if c > 0:
            second(c - 1)
    drain(q, s_w + s_a + s_x + [s_bc, s_y, s_ho])
    q.emit(nc)


def phase_mlp(nc, A, gd, hth, htl, y1, y2, of, W_fc1, b_fc1, W_fc2):
    NT = FF // 2 // 128
    FH = FF // 2
    q = Queues()
    wh = A.sb("wh", [128, 4, FH], R)
    wl = A.sb("wl", [128, 4, FH], R)
    wm = A.sb("wm", [128, FH], R)
    wr = A.sb("wr", [128, FH], R)
    vh = A.sb("vh", [128, NT, C], R)
    vl = A.sb("vl", [128, NT, C], R)
    stg = [A.sb(f"stg{i}", [128, FH]) for i in range(2)]
    b1 = A.sb("b1", [128, FF // 128])
    gt = A.sb("gt", [128, 2, C])
    hh = [A.sb(f"hh{i}", [128, KT, CH], R) for i in range(2)]
    hl = [A.sb(f"hl{i}", [128, 4, CH], R) for i in range(2)]
    af = [A.sb(f"af{i}", [128, CH]) for i in range(2)]
    ah = A.sb("ah", [128, NT, CH], R)
    al = A.sb("al", [128, NT, CH], R)
    yi = [A.sb(f"yi{i}", [128, C]) for i in range(2)]
    ug = [A.sb(f"ug{i}", [128, HALF]) for i in range(2)]
    pf = [A.ps(f"pf{i}", [128, 512]) for i in range(4)]
    pm = [A.ps(f"pm{i}", [128, 512]) for i in range(4)]
    s_w = [A.sem(f"w{i}") for i in range(2)]
    s_whi, s_wlo, s_z, s_c = A.sem("whi"), A.sem("wlo"), A.sem("z"), A.sem("c")
    s_h = [A.sem(f"h{i}") for i in range(2)]
    s_yi = [A.sem(f"yi{i}") for i in range(2)]
    s_yo = [A.sem(f"yo{i}") for i in range(2)]
    s_f1, s_af, s_ah, s_al, s_f2, s_ug, s_y = (A.sem("f1"), A.sem("af"), A.sem("ah"), A.sem("al"), A.sem("f2"),
                                               A.sem("ug"), A.sem("y"))
    for b in range(2):
        q.put("sync", lambda e, b=b: e.dma_start(gt[:, b, :], gd[1, b, :].partition_broadcast(128)), (), s_c, 16)
    tc = q.put("sync", lambda e: e.dma_start(b1[:, :], b_fc1.rearrange("(f p) -> p f", p=128),
                                             allow_slow_non_contiguous=True), (), s_c, 16)
    free = {"h": [None, None], "pf": [None] * 4, "pm": [None] * 4, "af": [None, None], "a": None,
            "yi": [None, None], "ug": [None, None]}
    th = {}
    n_pf, n_pm, n_ug, n_y = [0], [0], [0], [0]
    stfree = [None, None]
    mid = {}
    wrote = {}

    def load(n):
        i, c = n % 2, n % NCH
        rows = slice(c * CH, (c + 1) * CH)
        q.put("sync", lambda e: e.dma_start(hh[i][:, :, :].bitcast(F), hth[:, :, rows].rearrange("k p t -> p k t")),
              (free["h"][i],), s_h[i], 16)
        th[n] = q.put("sync", lambda e: e.dma_start(hl[i][:, :, :].bitcast(F),
                                                    htl[:, :, rows].rearrange("k p t -> p k t")),
                      (free["h"][i],), s_h[i], 16)

    def weights(half, wfree):
        for i in range(2):
            stfree[i] = stfree[i] or wfree
        if wfree is not None:
            for eng in ("scalar", "vector"):
                q.q[eng].append(([wfree], lambda e: None, None, 0))
        t1 = split_rows(q, A, W_fc1, wh, wl, wm, wr, half * FH, FH, stg, s_w, s_whi, s_wlo, s_z, stfree)
        for k in range(NT):
            i = (k + 1) % 2
            r0 = half * FH + k * 128
            ld = q.put("sync", lambda e, k=k, i=i, r0=r0: e.dma_start(stg[i][:, 0:C], W_fc2[r0:r0 + 128, :]),
                       (stfree[i],), s_w[i], 16)
            hi = q.put("scalar", lambda e, k=k, i=i: e.activation(vh[:, k, :], stg[i][:, 0:C], ACT.Copy), (ld,), s_whi)
            lo = q.put("vector", lambda e, k=k, i=i: e.tensor_tensor(
                vl[:, k, :], stg[i][:, 0:C], vh[:, k, :].bitcast(F), ALU.subtract), (ld, hi), s_wlo)
            stfree[i] = lo
        return t1, [lo, hi]

    load(0)
    for n in range(2 * NCH):
        half, c = n // NCH, n % NCH
        i, b = n % 2, c // (NCH // 2)
        if c == 0:
            tw1, tw2 = weights(half, s_f2.now() if half else None)
        if n + 1 < 2 * NCH:
            load(n + 1)
        for f in range(NT):
            m, j = n_pf[0] % 4, n_pf[0] % 2
            n_pf[0] += 1
            for k, (w, a) in enumerate(passes(wh, wl, wm, wr, hh[i], hl[i], slice(f * 128, f * 128 + 128),
                                              slice(0, CH))):
                tm = q.put("tensor", lambda e, w=w, a=a, k=k, m=m: e.matmul(
                    pf[m][:, :], w, a, start=k == 0, stop=k == 13),
                    tw1 + [th[n], free["pf"][m]], s_f1 if k == 13 else None)
            ta = q.put("scalar", lambda e, f=f, j=j, m=m, half=half: e.activation(
                af[j][:, :], pf[m][:, :], ACT.Gelu_apprx_tanh, bias=b1[:, half * NT + f:half * NT + f + 1]),
                (tm, tc, free["af"][j]), s_af)
            free["pf"][m] = ta
            tah = q.put("vector", lambda e, f=f, j=j: e.tensor_copy(ah[:, f, :], af[j][:, :]), (ta, free["a"]), s_ah)
            tal = q.put("vector", lambda e, f=f, j=j: e.tensor_tensor(
                al[:, f, :], af[j][:, :], ah[:, f, :].bitcast(F), ALU.subtract), (tah, free["a"]), s_al)
            free["af"][j] = tal
            mid[f] = [tah, tal]
        free["h"][i] = tm
        dst = y2 if half == 0 else of
        src = y1 if half == 0 else y2
        for t in range(4):
            y = n_y[0] % 2
            n_y[0] += 1
            r0 = c * CH + t * 128
            ty = q.put("sync", lambda e, y=y, r0=r0, src=src: e.dma_start(yi[y][:, :], src[r0:r0 + 128, :]),
                       (free["yi"][y], wrote.get(r0)), s_yi[y], 16)
            for n2 in range(2):
                m, k = n_pm[0] % 4, n_ug[0] % 2
                n_pm[0] += 1
                n_ug[0] += 1
                cs, ts = slice(n2 * HALF, (n2 + 1) * HALF), slice(t * 128, t * 128 + 128)
                for f in range(NT):
                    for p, (w, a) in enumerate(((ah[:, f, ts], vh[:, f, cs]), (ah[:, f, ts], vl[:, f, cs]),
                                                (al[:, f, ts], vh[:, f, cs]))):
                        end = f == NT - 1 and p == 2
                        tm = q.put("tensor", lambda e, w=w, a=a, f=f, p=p, m=m, end=end: e.matmul(
                            pm[m][:, 0:HALF], w, a, start=f == 0 and p == 0, stop=end),
                            tw2 + mid[f] + [free["pm"][m]], s_f2 if end else None)
                tu = q.put("vector", lambda e, m=m, k=k, cs=cs, b=b: e.tensor_tensor(
                    ug[k][:, :], pm[m][:, 0:HALF], gt[:, b, cs], ALU.mult), (tm, tc, free["ug"][k]), s_ug)
                free["pm"][m] = tu
                tyo = q.put("vector", lambda e, y=y, k=k, cs=cs: e.tensor_tensor(
                    yi[y][:, cs], ug[k][:, :], yi[y][:, cs], ALU.add), (tu, ty), s_y)
                free["ug"][k] = tyo
            free["yi"][y] = q.put("sync", lambda e, y=y, r0=r0, dst=dst: e.dma_start(dst[r0:r0 + 128, :],
                                                                                     yi[y][:, :]),
                                  (tyo,), s_yo[y], 16)
            wrote[r0] = free["yi"][y]
        free["a"] = tm
    drain(q, s_w + s_h + s_yi + s_yo + [s_c])
    q.emit(nc)


_INS = ["x", "cond_1152", "L0_cond_W_qkv", "L0_cond_b_qkv", "L0_cond_W_proj", "L0_cond_b_proj", "L0_cond_W_fc1",
        "L0_cond_b_fc1", "L0_cond_W_fc2", "L0_cond_b_fc2", "L0_cond_W_ada", "L0_cond_b_ada"]


def kernel(**inputs):
    import concourse.bacc as bacc
    from concourse.bass_utils import run_bass_kernel_spmd

    nc = bacc.Bacc("TRN2", target_bir_lowering=False, num_devices=1)
    arrays, args = {}, []
    for name in _INS:
        a = np.ascontiguousarray(inputs[name])
        arrays[f"in_{name}"] = a
        args.append(nc.dram_tensor(f"in_{name}", a.shape, mybir.dt.from_np(a.dtype), kind="ExternalInput").ap())
    args.append(nc.dram_tensor("out_0", (B, L, C), F, kind="ExternalOutput").ap())
    program(nc, *args)
    r = run_bass_kernel_spmd(nc, [arrays], core_ids=[0])
    return r.results[0]["out_0"]
```

```python
from contextlib import ExitStack

import numpy as np

import concourse.bass as bass
from concourse import mybir

F = mybir.dt.float32
R = mybir.dt.float32r
ALU = mybir.AluOpType
ACT = mybir.ActivationFunctionType
AX = mybir.AxisListType

B = 2
L = 2048
C = 576
H = 16
D = 36
FF = 2304
T = B * L
EPS = 1e-6
SCALE = float(D) ** -0.5
CH = 512
NCH = T // CH
KT = 5
NF = 2 * C // 128
HALF = C // 2
VW = 64 + D + 1
SPLIT = (0, 1, 2, 4, 5, 6, 8, 9, 10, 12, 13, 14)
ON_POOL = (2, 6, 10, 14)


class Counter:

    def __init__(self, sem):
        self.sem = sem
        self.n = 0

    def now(self):
        return (self, self.n)


class Queues:

    def __init__(self):
        self.q = {e: [] for e in ("sync", "tensor", "vector", "scalar", "gpsimd")}

    def put(self, eng, fn, waits=(), inc=None, by=1):
        if inc is not None:
            inc.n += by
        self.q[eng].append(([w for w in waits if w is not None], fn, inc, by))
        return inc.now() if inc is not None else None

    def run(self, eng, e):
        seen = {}
        for waits, fn, inc, by in self.q[eng]:
            for c, v in waits:
                if v > 0 and seen.get(c, 0) < v:
                    e.wait_ge(c.sem, v)
                    seen[c] = v
            ins = fn(e)
            if inc is not None:
                ins.then_inc(inc.sem, by)

    def emit(self, nc):
        with nc.Block() as block:
            for name in self.q:
                def body(e, name=name):
                    self.run(name, e)
                blocks = {"sync": block.sync, "tensor": block.tensor, "vector": block.vector,
                                "scalar": block.scalar, "gpsimd": block.gpsimd}
                blocks[name](body)


class Scope:

    def __init__(self, nc, ctx, tag, sems):
        self.nc, self.ctx, self.tag, self.sems = nc, ctx, tag, sems

    def sb(self, name, shape, dt=F):
        return self.ctx.enter_context(self.nc.sbuf_tensor(f"{self.tag}_{name}", shape, dt))

    def ps(self, name, shape):
        return self.ctx.enter_context(self.nc.psum_tensor(f"{self.tag}_{name}", shape, F))

    def sem(self, name):
        return Counter(self.sems.enter_context(self.nc.semaphore(f"{self.tag}_s_{name}")))


def drain(q, counters):
    for c in counters:
        q.q["sync"].append(([c.now()], lambda e: None, None, 0))


def finish(q):
    out = q.q["sync"]
    while out and out[-1][2] is None:
        out.pop()


def split_rows(q, s, W, wh, wl, wm, wr, c0, nc_, stg, s_ld, s_hi, s_lo, s_z, free):
    toks = []
    z = q.put("vector", lambda e: e.memset(wr[64:128, :].bitcast(F), 0.0), (), s_z)
    for kt in range(KT):
        b = kt % 2
        w = stg[b]
        if kt < 4:
            ld = q.put("sync", lambda e, kt=kt, w=w: e.dma_start(w[:, 0:nc_], W[kt * 128:kt * 128 + 128, c0:c0 + nc_]),
                       (free[b],), s_ld[b], 16)
            hi = q.put("scalar", lambda e, kt=kt, w=w: e.activation(wh[:, kt, :], w[:, 0:nc_], ACT.Copy), (ld,), s_hi)
            lo = q.put("vector", lambda e, kt=kt, w=w: e.tensor_tensor(
                wl[:, kt, :], w[:, 0:nc_], wh[:, kt, :].bitcast(F), ALU.subtract), (ld, hi), s_lo)
        else:
            q.put("sync", lambda e, w=w: e.dma_start(w[0:64, 0:nc_], W[512:576, c0:c0 + nc_]), (free[b],), s_ld[b], 16)
            ld = q.put("sync", lambda e, w=w: e.dma_start(w[64:128, 0:nc_], W[512:576, c0:c0 + nc_]), (free[b],),
                       s_ld[b], 16)
            hi = q.put("scalar", lambda e, w=w: e.activation(wm[:, :], w[:, 0:nc_], ACT.Copy), (ld,), s_hi)
            lo = q.put("vector", lambda e, w=w: e.tensor_tensor(
                wr[0:64, :], w[0:64, 0:nc_], wm[0:64, :].bitcast(F), ALU.subtract), (ld, hi), s_lo)
        free[b] = lo
        toks += [lo, hi]
    return [toks[-2], toks[-1], z]


def passes(wh, wl, wm, wr, hh, lo, wsl, tsl):
    out = []
    for kt in range(4):
        out += [(wh[:, kt, wsl], hh[:, kt, tsl]), (wh[:, kt, wsl], lo[:, kt, tsl]), (wl[:, kt, wsl], hh[:, kt, tsl])]
    out += [(wm[:, wsl], hh[:, 4, tsl]), (wr[:, wsl], hh[:, 4, tsl])]
    return out


def passes_t(wh, wl, wm, wr, hh, lo, wsl, tsl):
    out = []
    for kt in range(4):
        out += [(hh[:, kt, tsl], wh[:, kt, wsl]), (hh[:, kt, tsl], wl[:, kt, wsl]), (lo[:, kt, tsl], wh[:, kt, wsl])]
    out += [(hh[:, 4, tsl], wm[:, wsl]), (hh[:, 4, tsl], wr[:, wsl])]
    return out


def program(nc, x, cond, W_qkv, b_qkv, W_proj, b_proj, W_fc1, b_fc1, W_fc2, b_fc2, W_ada, b_ada, out):
    xf = x.rearrange("b l c -> (b l) c")
    of = out.rearrange("b l c -> (b l) c")

    def dram(name, shape):
        return nc.dram_tensor(name, shape, F, kind="Internal").ap()

    qkh = dram("qkh", [2 * C, T])
    qkl = dram("qkl", [2 * C, T])
    vd = dram("vd", [T, H * (D + 1)])
    aod = dram("aod", [T, C])
    hth = dram("hth", [KT, 128, T])
    htl = dram("htl", [4, 128, T])
    y1 = dram("y1", [T, C])
    y2 = dram("y2", [T, C])
    gd = dram("gd", [2, 2, C])

    with ExitStack() as top:
        P = Scope(nc, top, "g", top)
        ident = P.sb("ident", [128, 128])
        adaT = P.sb("adaT", [128, 6, KT, 2])
        eps = P.sb("eps", [128, 1])
        bq = P.sb("bq", [128, NF])

        with ExitStack() as ctx:
            A = Scope(nc, ctx, "a", top)
            wh = A.sb("wh", [128, 4, 3 * C], R)
            wl = A.sb("wl", [128, 4, 3 * C], R)
            wm = A.sb("wm", [128, 3 * C], R)
            wr = A.sb("wr", [128, 3 * C], R)
            phase_setup(nc, P, ident, adaT, eps, bq, gd, wh, wl, wm, wr, cond, W_ada, b_ada, W_qkv, b_qkv)
            phase_qkv(nc, A, ident, adaT, eps, bq, wh, wl, wm, wr, xf, b_qkv, qkh, qkl, vd)
        with ExitStack() as ctx:
            phase_attention(nc, Scope(nc, ctx, "b", top), ident, qkh, qkl, vd, aod)
        with ExitStack() as ctx:
            phase_proj(nc, Scope(nc, ctx, "c", top), ident, adaT, eps, gd, xf, aod, W_proj, b_proj, b_fc2, hth, htl, y1)
        with ExitStack() as ctx:
            phase_mlp(nc, Scope(nc, ctx, "d", top), gd, hth, htl, y1, y2, of, W_fc1, b_fc1, W_fc2)


def phase_setup(nc, P, ident, adaT, eps, bq, gd, wh, wl, wm, wr, cond, W_ada, b_ada, W_qkv, b_qkv):
    NA = 6 * C // 8
    with ExitStack() as ctx:
        S = Scope(nc, ctx, "s", P.sems)
        q = Queues()
        wa = S.sb("wa", [128, KT, 6 * C])
        cT = S.sb("cT", [128, KT, 2])
        ex = S.sb("ex", [128, KT, 2])
        e1 = S.sb("e1", [128, KT, 2])
        rc = S.sb("rc", [128, KT, 2])
        sc = S.sb("sc", [128, KT, 2])
        bad = S.sb("bad", [2, 6 * C])
        row = S.sb("row", [2, 6, 640])
        stg = [S.sb(f"stg{i}", [128, 3 * C]) for i in range(2)]
        ps = S.ps("ps", [128, 8, 512])
        s_c, s_b, s_bq, s_g = S.sem("c"), S.sem("b"), S.sem("bq"), S.sem("g")
        s_id, s_z, s_zz = S.sem("id"), S.sem("z"), S.sem("zz")
        s_wa = [S.sem(f"wa{k}") for k in range(KT)]
        s_si, s_mm, s_row, s_tr, s_ad = S.sem("si"), S.sem("mm"), S.sem("row"), S.sem("tr"), S.sem("ad")
        s_ld = [S.sem(f"ld{i}") for i in range(2)]
        s_hi, s_lo = S.sem("hi"), S.sem("lo")

        q.put("gpsimd", lambda e: e.memset(ident[:, :], 0.0), (), s_id)
        tid = q.put("gpsimd", lambda e: e.affine_select(
            out=ident[:, :], in_=ident[:, :], compare_op=ALU.not_equal, fill=1.0, base=0, pattern=[[-1, 128]],
            channel_multiplier=1), (s_id.now(),), s_id)
        zc = q.put("vector", lambda e: e.memset(cT[:, :, :], 0.0), (), s_z)
        q.put("vector", lambda e: e.memset(eps[:, :], EPS), (), s_zz)
        for b in range(2):
            q.put("sync", lambda e, b=b: e.dma_start(cT[:, 0:4, b], cond[b, 0:512].rearrange("(k p) -> p k", p=128),
                                                  allow_slow_non_contiguous=True),
                  (zc,), s_c, 16)
            tc = q.put("sync", lambda e, b=b: e.dma_start(cT[0:64, 4, b:b + 1],
                                                         cond[b, 512:576].rearrange("(p o) -> p o", o=1),
                                                         allow_slow_non_contiguous=True),
                       (zc,), s_c, 16)
        for kt in range(KT):
            n = 128 if kt < 4 else 64
            q.put("sync", lambda e, kt=kt, n=n: e.dma_start(wa[0:n, kt, :], W_ada[kt * 128:kt * 128 + n, :]), (),
                  s_wa[kt], 16)
        for b in range(2):
            tb = q.put("sync", lambda e, b=b: e.dma_start(bad[b:b + 1, :], b_ada.rearrange("(o n) -> o n", o=1)), (),
                       s_b, 16)
        q.put("sync", lambda e: e.dma_start(bq[:, :], b_qkv[0:2 * C].rearrange("(f p) -> p f", p=128),
                                            allow_slow_non_contiguous=True), (), s_bq, 16)

        t = q.put("scalar", lambda e: e.activation(ex[:, :, :], cT[:, :, :], ACT.Exp, scale=-1.0), (tc,), s_si)
        t = q.put("vector", lambda e: e.tensor_scalar(e1[:, :, :], ex[:, :, :], 1.0, None, ALU.add), (t,), s_si)
        t = q.put("vector", lambda e: e.reciprocal(rc[:, :, :], e1[:, :, :]), (t,), s_si)
        t = q.put("vector", lambda e: e.tensor_tensor(sc[:, :, :], cT[:, :, :], rc[:, :, :], ALU.mult), (t, tc), s_si)
        for kt in range(KT):
            n = 128 if kt < 4 else 64
            for j in range(8):
                tm = q.put("tensor", lambda e, kt=kt, n=n, j=j: e.matmul(
                    ps[0:2, j, 0:NA], sc[0:n, kt, :], wa[0:n, kt, j * NA:(j + 1) * NA], start=kt == 0,
                    stop=kt == KT - 1), (t, (s_wa[kt], 16)), s_mm)
        tr = None
        for v in range(6):
            for a, b_ in ((0, C),):
                lo_, hi_ = v * C, v * C + C
                while lo_ < hi_:
                    j = lo_ // NA
                    m = min(hi_, (j + 1) * NA)
                    tr = q.put("vector", lambda e, v=v, lo_=lo_, m=m, j=j: e.tensor_tensor(
                        row[:, v, lo_ - v * C:m - v * C], ps[0:2, j, lo_ - j * NA:m - j * NA], bad[:, lo_:m], ALU.add),
                        (tm, tb), s_row)
                    lo_ = m
            tr = q.put("vector", lambda e, v=v: e.tensor_copy(row[:, v, C:640], row[:, v, 512:C]), (tr,), s_row)
        for g, v in enumerate((2, 5)):
            tg = q.put("sync", lambda e, g=g, v=v: e.dma_start(gd[g, :, :], row[:, v, 0:C]), (tr,), s_g, 16)
        for v in range(6):
            for kt in range(KT):
                tt = q.put("tensor", lambda e, v=v, kt=kt: e.transpose(
                    ps[:, 0, (v * KT + kt) * 2:(v * KT + kt) * 2 + 2], row[:, v, kt * 128:kt * 128 + 128],
                    ident[0:2, 0:2]), (tr, tid), s_tr)
        ta = q.put("vector", lambda e: e.tensor_copy(adaT[:, :, :, :].rearrange("p v k b -> p (v k b)"),
                                                     ps[:, 0, 0:60]), (tt,), s_ad)
        for v in (1, 4):
            q.put("vector", lambda e, v=v: e.tensor_scalar(adaT[:, v, :, :], adaT[:, v, :, :], 1.0, None, ALU.add),
                  (ta,), s_ad)
        split_rows(q, S, W_qkv, wh, wl, wm, wr, 0, 3 * C, stg, s_ld, s_hi, s_lo, s_zz, [None, None])
        drain(q, [s_c, s_b, s_bq, s_g] + s_ld)
        q.emit(nc)


def phase_qkv(nc, A, ident, adaT, eps, bq, wh, wl, wm, wr, xf, b_qkv, qkh, qkl, vd):
    q = Queues()
    xin = [A.sb(f"x{i}", [128, 4, C]) for i in range(2)]
    xn = A.sb("xn", [128, 4, 640])
    st = A.sb("st", [128, 4, 2, 6])
    mv = A.sb("mv", [128, 4, 2])
    sd = A.sb("sd", [128, 4])
    rs = A.sb("rs", [128, 4])
    hf = [A.sb(f"hf{i}", [128, CH]) for i in range(2)]
    hh = [A.sb(f"hh{i}", [128, KT, CH], R) for i in range(2)]
    lo = [A.sb(f"lo{i}", [128, 4, CH], R) for i in range(2)]
    tf = [A.sb(f"tf{i}", [128, CH]) for i in range(2)]
    th = [A.sb(f"th{i}", [128, CH], R) for i in range(2)]
    tl = [A.sb(f"tl{i}", [128, CH], R) for i in range(2)]
    vc = [A.sb(f"vc{i}", [128, 4, H, D + 1]) for i in range(2)]
    bv = A.sb("bv", [128, C])
    pt = [A.ps(f"pt{i}", [128, 512]) for i in range(2)]
    pm = [A.ps(f"pm{i}", [128, 512]) for i in range(4)]
    s_x = [A.sem(f"x{i}") for i in range(2)]
    s_bv, s_st, s_sd, s_rs, s_xn = A.sem("bv"), A.sem("st"), A.sem("sd"), A.sem("rs"), A.sem("xn")
    s_tp, s_hf, s_hh, s_lo = A.sem("tp"), A.sem("hf"), A.sem("hh"), A.sem("lo")
    s_mm, s_tf, s_tl, s_vc, s_on = A.sem("mm"), A.sem("tf"), A.sem("tl"), A.sem("vc"), A.sem("on")
    s_qo = [A.sem(f"qo{i}") for i in range(2)]
    s_vo = [A.sem(f"vo{i}") for i in range(2)]

    tbv = q.put("sync", lambda e: e.dma_start(bv[:, :], b_qkv[2 * C:3 * C].partition_broadcast(128)), (), s_bv, 16)
    for i in range(2):
        ton = q.put("vector", lambda e, i=i: e.memset(vc[i][:, :, :, D:D + 1].rearrange("p t h o -> p (t h) o"), 1.0),
                    (), s_on)
    free = {"x": [None, None], "xn": None, "pt": [None, None], "hf": [None, None], "h": [None, None],
            "pm": [None] * 4, "tf": [None, None], "tl": [None, None], "vc": [None, None], "rs": None}
    ready = {}
    n_pt = [0]
    n_pm = [0]

    def load(c):
        i = c % 2
        return q.put("sync", lambda e: e.dma_start(
            xin[i][:, :, :], xf[c * CH:(c + 1) * CH, :].rearrange("(t p) c -> p t c", p=128)), (free["x"][i],),
            s_x[i], 16)

    def prepare(c):
        i, b = c % 2, c // (NCH // 2)
        tx = load(c)
        yield
        for t in range(4):
            for g in range(2):
                ts = q.put("vector", lambda e, t=t, g=g: e.bn_stats(
                    st[:, t, g, :], xin[i][:, t, g * HALF:(g + 1) * HALF]), (tx, free["rs"]), s_st)
            ts = q.put("vector", lambda e, t=t: e.bn_aggr(mv[:, t, :], st[:, t, :, :]), (ts, free["xn"]), s_st)
        tsd = q.put("scalar", lambda e: e.activation(sd[:, :], mv[:, :, 1], ACT.Sqrt, bias=eps[:, 0:1]), (ts,), s_sd)
        trs = q.put("vector", lambda e: e.reciprocal(rs[:, :], sd[:, :]), (tsd,), s_rs)
        free["rs"] = trs
        yield
        for t in range(4):
            for a, z, d in ((0, C, 0), (512, C, C)):
                txn = q.put("vector", lambda e, t=t, a=a, z=z, d=d: e.tensor_scalar(
                    xn[:, t, d:d + z - a], xin[i][:, t, a:z], mv[:, t, 0:1], rs[:, t:t + 1], ALU.subtract, ALU.mult),
                    (trs, free["xn"]), s_xn)
            if t == 1:
                yield
        free["x"][i] = txn
        yield
        for kt in range(KT):
            j = n_pt[0] % 2
            n_pt[0] += 1
            for t in range(4):
                ttp = q.put("tensor", lambda e, t=t, kt=kt, j=j: e.transpose(
                    pt[j][:, t * 128:t * 128 + 128], xn[:, t, kt * 128:kt * 128 + 128], ident[:, :]),
                    (txn, free["pt"][j]), s_tp)
            thf = q.put("scalar", lambda e, kt=kt, j=j: e.activation(
                hf[j][:, :], pt[j][:, :], ACT.Identity, bias=adaT[:, 0, kt, b:b + 1], scale=adaT[:, 1, kt, b:b + 1]),
                (ttp, free["hf"][j]), s_hf)
            free["pt"][j] = thf
            thh = q.put("vector", lambda e, kt=kt, j=j: e.tensor_copy(hh[i][:, kt, :], hf[j][:, :]),
                        (thf, free["h"][i]), s_hh)
            if kt < 4:
                tlo = q.put("vector", lambda e, kt=kt, j=j: e.tensor_tensor(
                    lo[i][:, kt, :], hf[j][:, :], hh[i][:, kt, :].bitcast(F), ALU.subtract), (thh, free["h"][i]), s_lo)
            else:
                tlo = q.put("vector", lambda e, kt=kt, j=j: e.tensor_tensor(
                    hh[i][64:128, kt, :], hf[j][64:128, :], hh[i][64:128, kt, :].bitcast(F), ALU.subtract),
                    (thh,), s_lo)
            free["hf"][j] = tlo
            yield
        free["xn"] = ttp
        ready[c] = [thh, tlo]

    for _ in prepare(0):
        pass
    for c in range(NCH):
        i = c % 2
        nxt = prepare(c + 1) if c + 1 < NCH else iter(())
        for f in range(NF):
            m, j = n_pm[0] % 4, f % 2
            n_pm[0] += 1
            ps_ = passes(wh, wl, wm, wr, hh[i], lo[i], slice(f * 128, f * 128 + 128), slice(0, CH))
            for n, (w, a) in enumerate(ps_):
                tm = q.put("tensor", lambda e, w=w, a=a, n=n, m=m: e.matmul(
                    pm[m][:, :], w, a, start=n == 0, stop=n == 13),
                    ready[c] + [free["pm"][m]], s_mm if n == 13 else None)
            tt = q.put("scalar", lambda e, f=f, j=j, m=m: e.activation(
                tf[j][:, :], pm[m][:, :], ACT.Identity, bias=bq[:, f:f + 1]), (tm, free["tf"][j]), s_tf)
            tt = q.put("scalar", lambda e, f=f, j=j, m=m: e.activation(
                th[j][:, :], pm[m][:, :], ACT.Identity, bias=bq[:, f:f + 1]), (tm, free["tl"][j]), s_tf)
            free["pm"][m] = tt
            tlw = q.put("vector", lambda e, j=j: e.tensor_tensor(
                tl[j][:, :], tf[j][:, :], th[j][:, :].bitcast(F), ALU.subtract), (tt, free["tl"][j]), s_tl)
            free["tf"][j] = tlw
            q.put("sync", lambda e, f=f, j=j, c=c: e.dma_start(
                qkh[f * 128:f * 128 + 128, c * CH:(c + 1) * CH], th[j][:, :].bitcast(F)), (tt,), s_qo[j], 16)
            free["tl"][j] = q.put("sync", lambda e, f=f, j=j, c=c: e.dma_start(
                qkl[f * 128:f * 128 + 128, c * CH:(c + 1) * CH], tl[j][:, :].bitcast(F)), (tlw,), s_qo[j], 16)
            next(nxt, None)
        for t in range(4):
            for n2 in range(2):
                m = n_pm[0] % 4
                n_pm[0] += 1
                ps_ = passes_t(wh, wl, wm, wr, hh[i], lo[i], slice(2 * C + n2 * HALF, 2 * C + (n2 + 1) * HALF),
                               slice(t * 128, t * 128 + 128))
                for n, (w, a) in enumerate(ps_):
                    tm = q.put("tensor", lambda e, w=w, a=a, n=n, m=m: e.matmul(
                        pm[m][:, 0:HALF], w, a, start=n == 0, stop=n == 13),
                        ready[c] + [free["pm"][m]], s_mm if n == 13 else None)
                tv = q.put("vector", lambda e, t=t, n2=n2, m=m, i=i: e.tensor_tensor(
                    vc[i][:, t, n2 * 8:n2 * 8 + 8, 0:D], pm[m][:, 0:HALF].rearrange("p (h d) -> p h d", d=D),
                    bv[:, n2 * HALF:(n2 + 1) * HALF].rearrange("p (h d) -> p h d", d=D), ALU.add),
                    (tm, tbv, ton, free["vc"][i]), s_vc)
                free["pm"][m] = tv
            next(nxt, None)
        free["h"][i] = tm
        free["vc"][i] = q.put("sync", lambda e, i=i, c=c: e.dma_start(
            vd[c * CH:(c + 1) * CH, :].rearrange("(t p) n -> p t n", p=128),
            vc[i][:, :, :, :].rearrange("p t h d -> p t (h d)")), (tv, ton), s_vo[i], 16)
        for _ in nxt:
            pass
    drain(q, s_qo + s_vo + s_x + [s_bv])
    q.emit(nc)


def phase_attention(nc, A, ident, qkh, qkl, vd, aod):
    q = Queues()
    NB = 3
    NH = B * H
    qs = [A.sb(f"qs{i}", [128, L], R) for i in range(NB)]
    ks = [A.sb(f"ks{i}", [128, L], R) for i in range(NB)]
    vf = [A.sb(f"vf{i}", [128, 16, VW]) for i in range(2)]
    vs = [A.sb(f"vs{i}", [128, 16, VW], R) for i in range(2)]
    NP = 7
    NR = 6
    pt = [A.sb(f"pt{i}", [128, 1024]) for i in range(NP)]
    ph = [A.sb(f"ph{i}", [128, 1024], R) for i in range(NR)]
    pl = [A.sb(f"pl{i}", [128, 1024], R) for i in range(NR)]
    oa = A.sb("oa", [D + 1, 1024])
    ob = A.sb("ob", [D + 1, 1024])
    oc = A.sb("oc", [D + 1, 1024])
    rc = A.sb("rc", [128, 8])
    ao = [A.sb(f"ao{i}", [128, 8, D]) for i in range(2)]
    mx = A.sb("mx", [128, 16, 4])
    nm = A.sb("nm", [128, 16])
    mh = A.sb("mh", [16, 128], R)
    ml = A.sb("ml", [16, 128], R)
    st = [A.ps(f"st{i}", [128, 1024]) for i in range(2)]
    op = A.ps("op", [128, 1024])
    sp = [A.ps(f"sp{i}", [128, 512]) for i in range(2)]
    s_qk = [A.sem(f"qk{i}") for i in range(NB)]
    s_v = [A.sem(f"v{i}") for i in range(2)]
    s_m = [A.sem(f"m{i}") for i in range(NB)]
    s_ao = [A.sem(f"ao{i}") for i in range(2)]
    s_ini, s_vs, s_s, s_mx, s_nm, s_mt, s_mh = (A.sem("ini"), A.sem("vs"), A.sem("s"), A.sem("mx"), A.sem("nm"),
                                                A.sem("mt"), A.sem("mh"))
    s_plg = A.sem("plg")
    s_st, s_p, s_ph, s_pl, s_pv = A.sem("st"), A.sem("p"), A.sem("ph"), A.sem("pl"), A.sem("pv")
    s_oe, s_oc, s_ot, s_rc, s_an = A.sem("oe"), A.sem("oc"), A.sem("ot"), A.sem("rc"), A.sem("an")

    for i in range(NB):
        q.put("vector", lambda e, i=i: e.memset(ks[i][96:128, :].bitcast(F), 1.0), (), s_ini)
    for i in range(2):
        q.put("vector", lambda e, i=i: e.memset(vf[i][:, :, :], 0.0), (), s_ini)
        q.put("vector", lambda e, i=i: e.memset(vs[i][:, :, :].bitcast(F), 0.0), (), s_ini)
    ini = s_ini.now()

    free = {"qk": [None] * NB, "v": [None, None], "vs": [None, None], "st": [None, None], "pt": [None] * NP,
            "ph": [None] * NR, "sp": [None, None], "op": None, "mx": None, "nm": None, "mh": None,
            "oa": None, "oc": None, "rc": None, "ao": [None, None]}
    tqk, tv, tvs, tm_ = {}, {}, {}, {}
    n_sp, n_ph = [0], [0]

    def load(h):
        i, b, hd = h % NB, h // H, h % H
        sl = slice(b * L, (b + 1) * L)
        for dst, src, r in ((qs, qkh, 0), (qs, qkl, 36), (qs, qkh, 72), (ks, qkh, 0), (ks, qkh, 36), (ks, qkl, 72)):
            f0 = hd * D + (C if dst is ks else 0)
            tqk[h] = q.put("sync", lambda e, dst=dst, src=src, r=r, f0=f0: e.dma_start(
                dst[i][r:r + D, :].bitcast(F), src[f0:f0 + D, sl]), (ini, free["qk"][i]), s_qk[i], 16)

    def load_v(h):
        b, hd, v = h // H, h % H, h % 2
        sl = slice(b * L, (b + 1) * L)
        tv[h] = q.put("sync", lambda e: e.dma_start(
            vf[v][:, :, 0:D + 1],
            vd[sl, hd * (D + 1):(hd + 1) * (D + 1)].rearrange("(k p) d -> p k d", p=128)), (ini, free["v"][v]),
            s_v[v], 16)

    def split_v(h):
        v = h % 2
        t = q.put("vector", lambda e: e.tensor_copy(vs[v][:, :, 0:D + 1], vf[v][:, :, 0:D + 1]),
                  (ini, tv[h], free["v"][v]), s_vs)
        tvs[h] = q.put("vector", lambda e: e.tensor_tensor(
            vs[v][:, :, 64:VW], vf[v][:, :, 0:D + 1], vs[v][:, :, 0:D + 1].bitcast(F), ALU.subtract), (t,), s_vs)

    def slot():
        j = n_sp[0] % 2
        n_sp[0] += 1
        return j

    def score_max(h, n):
        qb, k4 = n // 4, n % 4
        i, j = h % NB, slot()
        t = q.put("tensor", lambda e: e.matmul(
            sp[j][:, :], qs[i][0:108, qb * 128:qb * 128 + 128], ks[i][0:108, k4 * 512:k4 * 512 + 512], start=True,
            stop=True), (tqk[h], free["sp"][j]), s_s)
        free["sp"][j] = q.put("vector", lambda e: e.tensor_reduce(mx[:, qb, k4:k4 + 1], sp[j][:, :], AX.X, ALU.max),
                              (t, free["mx"]), s_mx)

    def row_max(h):
        t = q.put("vector", lambda e: e.tensor_reduce(nm[:, :], mx[:, :, :], AX.X, ALU.max, negate=True),
                  (s_mx.now(), free["nm"]), s_nm)
        free["mx"] = t
        return t

    def max_rows(h, t):
        i, j = h % NB, slot()
        t = q.put("tensor", lambda e: e.transpose(sp[j][0:16, 0:128], nm[:, :], ident[:, :]), (t, free["sp"][j]), s_mt)
        free["nm"] = t
        t1 = q.put("vector", lambda e: e.tensor_copy(mh[:, :], sp[j][0:16, 0:128]), (t, free["mh"]), s_mh)
        t2 = q.put("vector", lambda e: e.tensor_tensor(ml[:, :], sp[j][0:16, 0:128], mh[:, :].bitcast(F),
                                                       ALU.subtract), (t1, free["mh"]), s_mh)
        free["sp"][j] = t2
        q.put("sync", lambda e: e.dma_start(qs[i][108:109, :].bitcast(F), mh[:, :].bitcast(F)),
              (t1,), s_m[i], 16)
        tm_[h] = q.put("sync", lambda e: e.dma_start(qs[i][109:110, :].bitcast(F), ml[:, :].bitcast(F)), (t2,),
                       s_m[i], 16)
        free["mh"] = tm_[h]

    pend = {}

    def scores_t(g):
        h, u, kb = g // 32, (g // 16) % 2, g % 16
        i, j = h % NB, g % 2
        for a in range(2):
            t = q.put("tensor", lambda e, a=a: e.matmul(
                st[j][:, a * 512:a * 512 + 512], ks[i][0:110, kb * 128:kb * 128 + 128],
                qs[i][0:110, u * 1024 + a * 512:u * 1024 + a * 512 + 512], start=True, stop=True),
                (ini, tqk[h], tm_[h], free["st"][j]), s_st if a else None)
        return t

    def exps(g, t):
        j, p = g % 2, g % NP
        tp = q.put("scalar", lambda e: e.activation(pt[p][:, :], st[j][:, :], ACT.Exp, scale=SCALE),
                   (t, free["pt"][p]), s_p)
        free["st"][j] = tp
        pend[g] = (None, tp, tp)

    def high(g):
        p, tp = g % NP, pend[g][1]
        r = n_ph[0] % NR
        n_ph[0] += 1
        th = q.put("scalar", lambda e: e.activation(ph[r][:, :], pt[p][:, :], ACT.Copy), (tp, free["ph"][r]), s_ph)
        pend[g] = (r, th, None)

    def low(g):
        p = g % NP
        r, th, _ = pend[g]
        pool = g % 16 in ON_POOL
        tl = q.put("gpsimd" if pool else "vector", lambda e: e.tensor_tensor(
            pl[r][:, :], pt[p][:, :], ph[r][:, :].bitcast(F), ALU.subtract), (th, free["ph"][r]),
            s_plg if pool else s_pl)
        free["pt"][p] = tl
        pend[g] = (r, th, tl)

    def pv(g):
        h, kb = g // 32, g % 16
        v, p = h % 2, g % NP
        r, t0, t1 = pend.pop(g)
        first, last = kb == 0, kb == 15
        if r is None:
            parts = [(vf[v][:, kb, :], pt[p], t0)]
        else:
            parts = [(vs[v][:, kb, :], ph[r], t0), (vs[v][:, kb, :], pl[r], t1)]
        for n, (w, m, tk) in enumerate(parts):
            for a in range(2):
                t = q.put("tensor", lambda e, w=w, m=m, a=a, n=n: e.matmul(
                    op[0:VW, a * 512:a * 512 + 512], w, m[:, a * 512:a * 512 + 512],
                    start=first and n == 0, stop=last and n == len(parts) - 1),
                    (tk, tvs[h], free["op"] if first else None), s_pv)
                if n == len(parts) - 1 and a == 1:
                    if r is None:
                        free["pt"][p] = t
                    else:
                        free["ph"][r] = t
                    if last and (g // 16) % 2 == 1:
                        free["v"][v] = t
                yield t

    def o_out(g, t):
        free["op_src"] = t
        q.put("scalar", lambda e: e.activation(oa[:, :], op[64:VW, :], ACT.Copy), (t, free["oa"]), s_oe)
        t = q.put("scalar", lambda e: e.activation(ob[:, :], op[0:D + 1, :], ACT.Copy), (t, free["oa"]), s_oe)
        free["op"] = t
        t = q.put("gpsimd", lambda e: e.tensor_tensor(oc[:, :], oa[:, :], ob[:, :], ALU.add), (t, free["oc"]), s_oc)
        free["oa"] = t
        return t

    def o_norm(g, t):
        h, u = g // 32, (g // 16) % 2
        b, hd = h // H, h % H
        j, k = slot(), (g // 16) % 2
        for n in range(8):
            tt = q.put("tensor", lambda e, n=n: e.transpose(sp[j][:, n * 37:n * 37 + 37], oc[:, n * 128:n * 128 + 128],
                                                            ident[0:37, 0:37]), (t, free["sp"][j]), s_ot)
        free["oc"] = tt
        view = sp[j][:, 0:296].rearrange("p (n d) -> p n d", d=37)
        t1 = q.put("vector", lambda e: e.reciprocal(rc[:, :], view[:, :, D]), (tt, free["rc"]), s_rc)
        t2 = q.put("vector", lambda e: e.tensor_tensor(
            ao[k][:, :, :], view[:, :, 0:D], rc[:, :].unsqueeze(2).to_broadcast([128, 8, D]), ALU.mult),
            (t1, free["ao"][k]), s_an)
        free["sp"][j] = t2
        free["rc"] = t2
        r0 = b * L + u * 1024
        free["ao"][k] = q.put("sync", lambda e: e.dma_start(
            aod[r0:r0 + 1024, hd * D:(hd + 1) * D].rearrange("(n p) d -> p n d", p=128), ao[k][:, :, :]), (t2,),
            s_ao[k], 16)

    load(0)
    load(1)
    load_v(0)
    split_v(0)
    G = NH * 32
    LAG = 4
    LEAD = 6
    todo = [0]

    def maxima(n, upto):
        while n > 0 and todo[0] < min(upto, NH * 64):
            h, k = divmod(todo[0], 64)
            score_max(h, k)
            todo[0] += 1
            n -= 1
            if k == 63:
                rows.append((h, row_max(h)))

    rows = []
    maxima(64 + 2 * LEAD, 64 + 2 * LEAD)
    max_rows(*rows.pop())
    done = {}
    for g in range(G + LAG + 4):
        h, s = g // 32, g % 32
        upto = 2 * (g + 1) + 64 + 2 * LEAD
        late = rows.pop() if rows else None
        if g < G:
            if s == 0 and h + 2 < NH:
                load(h + 2)
            if h + 1 < NH and s == LAG + 1:
                load_v(h + 1)
            t = scores_t(g)
            exps(g, t)
            if s == 31:
                free["qk"][h % NB] = t
        if 0 <= g - 1 < G and (g - 1) % 16 in SPLIT:
            high(g - 1)
        maxima(1, upto)
        tl = None
        now = []
        if 0 <= g - LAG < G and (g - LAG) % 16 == 1:
            now.append(g - LAG - 1)
        if 0 <= g - LAG < G and (g - LAG) % 16:
            now.append(g - LAG)
        for k in now:
            for n, tl in enumerate(pv(k)):
                if n == 0:
                    maxima(1, upto)
        maxima(1, upto)
        if 0 <= g - 2 < G and (g - 2) % 16 in SPLIT:
            low(g - 2)
        if late is not None:
            max_rows(*late)
        if tl is not None and (g - LAG) % 16 == 15:
            done[g + 3] = (g - LAG, o_out(g - LAG, tl))
        if g < G and h + 1 < NH and s == 16:
            split_v(h + 1)
        if g in done:
            o_norm(*done.pop(g))
    drain(q, s_ao + s_m + s_qk + s_v)
    q.emit(nc)


def phase_proj(nc, A, ident, adaT, eps, gd, xf, aod, W_proj, b_proj, b_fc2, hth, htl, y1):
    q = Queues()
    wh = A.sb("wh", [128, 4, C], R)
    wl = A.sb("wl", [128, 4, C], R)
    wm = A.sb("wm", [128, C], R)
    wr = A.sb("wr", [128, C], R)
    stg = [A.sb(f"stg{i}", [128, C]) for i in range(2)]
    gt = A.sb("gt", [128, 2, 2, C])
    bb = A.sb("bb", [128, 2, C])
    gb = A.sb("gb", [128, 2, 2, C])
    ai = [A.sb(f"ai{i}", [128, 4, 640]) for i in range(2)]
    xi = [A.sb(f"xi{i}", [128, 4, C]) for i in range(2)]
    x1 = [A.sb(f"x1{i}", [128, 4, C]) for i in range(2)]
    xo = A.sb("xo", [128, 4, C])
    ug = [A.sb(f"ug{i}", [128, HALF]) for i in range(2)]
    xn = A.sb("xn", [128, 4, 640])
    st = A.sb("st", [128, 4, 2, 6])
    mv = A.sb("mv", [128, 4, 2])
    sd = A.sb("sd", [128, 4])
    rs = A.sb("rs", [128, 4])
    ah = [A.sb(f"ah{i}", [128, KT, CH], R) for i in range(2)]
    al = [A.sb(f"al{i}", [128, 4, CH], R) for i in range(2)]
    hf = [A.sb(f"hf{i}", [128, CH]) for i in range(2)]
    hh = A.sb("hh", [128, KT, CH], R)
    hl = A.sb("hl", [128, 4, CH], R)
    pt = [A.ps(f"pt{i}", [128, 512]) for i in range(4)]
    pm = [A.ps(f"pm{i}", [128, 512]) for i in range(4)]
    s_w = [A.sem(f"w{i}") for i in range(2)]
    s_whi, s_wlo, s_z, s_bc, s_gb = A.sem("whi"), A.sem("wlo"), A.sem("z"), A.sem("bc"), A.sem("gb")
    s_a = [A.sem(f"a{i}") for i in range(2)]
    s_x = [A.sem(f"x{i}") for i in range(2)]
    s_tp, s_ah, s_al, s_mm, s_ug, s_xg, s_x1 = (A.sem("tp"), A.sem("ah"), A.sem("al"), A.sem("mm"), A.sem("ug"),
                                                A.sem("xg"), A.sem("xa"))
    s_st, s_sd, s_rs, s_xn, s_xo, s_hf, s_hh, s_hl = (A.sem("st"), A.sem("sd"), A.sem("rs"), A.sem("xn"), A.sem("xo"),
                                                      A.sem("hf"), A.sem("hh"), A.sem("hl"))
    s_y, s_ho = A.sem("y"), A.sem("ho")

    tw = split_rows(q, A, W_proj, wh, wl, wm, wr, 0, C, stg, s_w, s_whi, s_wlo, s_z, [None, None])
    for g in range(2):
        for b in range(2):
            q.put("sync", lambda e, g=g, b=b: e.dma_start(gt[:, g, b, :], gd[g, b, :].partition_broadcast(128)), (),
                  s_bc, 16)
    for g, src in enumerate((b_proj, b_fc2)):
        tbc = q.put("sync", lambda e, g=g, src=src: e.dma_start(bb[:, g, :], src.partition_broadcast(128)), (),
                    s_bc, 16)
    for g in range(2):
        for b in range(2):
            tgb = q.put("gpsimd", lambda e, g=g, b=b: e.tensor_tensor(gb[:, g, b, :], gt[:, g, b, :], bb[:, g, :],
                                                                      ALU.mult), (tbc,), s_gb)
    free = {"ai": [None, None], "xi": [None, None], "pt": [None] * 4, "pm": [None] * 4, "ah": [None, None], "ug": [None, None],
            "x1": [None, None], "xo": None, "xn": None, "rs": None, "hf": [None, None], "hh": None}
    n_pt, n_pm, n_ug = [0], [0], [0]
    tx1 = {}

    ta_, txg_, tah_ = {}, {}, {}

    def load(c):
        i = c % 2
        rows = slice(c * CH, (c + 1) * CH)
        q.put("sync", lambda e: e.dma_start(ai[i][:, :, 0:C], aod[rows, :].rearrange("(t p) c -> p t c", p=128)),
              (free["ai"][i],), s_a[i], 16)
        ta_[c] = q.put("sync", lambda e: e.dma_start(
            ai[i][:, :, C:640], aod[rows, 512:C].rearrange("(t p) c -> p t c", p=128)), (free["ai"][i],), s_a[i], 16)
        tx = q.put("sync", lambda e: e.dma_start(xi[i][:, :, :], xf[rows, :].rearrange("(t p) c -> p t c", p=128)),
                   (free["xi"][i],), s_x[i], 16)
        for t in range(4):
            txg_[c] = q.put("gpsimd", lambda e, t=t: e.tensor_tensor(
                xi[i][:, t, :], xi[i][:, t, :], gb[:, 0, c // (NCH // 2), :], ALU.add), (tx, tgb), s_xg)

    def turn(c):
        i = c % 2
        for kt in range(KT):
            j = n_pt[0] % 4
            n_pt[0] += 1
            for t in range(4):
                ttp = q.put("tensor", lambda e, t=t, kt=kt, j=j: e.transpose(
                    pt[j][:, t * 128:t * 128 + 128], ai[i][:, t, kt * 128:kt * 128 + 128], ident[:, :]),
                    (ta_[c], free["pt"][j]), s_tp)
            tah = q.put("scalar", lambda e, kt=kt, j=j: e.activation(ah[i][:, kt, :], pt[j][:, :], ACT.Copy),
                        (ttp, free["ah"][i]), s_ah)
            if kt < 4:
                tal = q.put("vector", lambda e, kt=kt, j=j: e.tensor_tensor(
                    al[i][:, kt, :], pt[j][:, :], ah[i][:, kt, :].bitcast(F), ALU.subtract), (tah, free["ah"][i]),
                    s_al)
            else:
                tal = q.put("vector", lambda e, kt=kt, j=j: e.tensor_tensor(
                    ah[i][64:128, kt, :], pt[j][64:128, :], ah[i][64:128, kt, :].bitcast(F), ALU.subtract), (tah,),
                    s_al)
            free["pt"][j] = tal
            if kt == KT - 1:
                free["ai"][i] = ttp
                tah_[c] = [tah, tal]
            yield

    def project(c):
        i, b = c % 2, c // (NCH // 2)
        for t in range(4):
            for n2 in range(2):
                m, k = n_pm[0] % 4, n_ug[0] % 2
                n_pm[0] += 1
                n_ug[0] += 1
                cs = slice(n2 * HALF, (n2 + 1) * HALF)
                for n, (w, a) in enumerate(passes_t(wh, wl, wm, wr, ah[i], al[i], cs, slice(t * 128, t * 128 + 128))):
                    tm = q.put("tensor", lambda e, w=w, a=a, n=n, m=m: e.matmul(
                        pm[m][:, 0:HALF], w, a, start=n == 0, stop=n == 13),
                        tw + tah_[c] + [free["pm"][m]], s_mm if n == 13 else None)
                tu = q.put("vector", lambda e, m=m, k=k, cs=cs: e.tensor_tensor(
                    ug[k][:, :], pm[m][:, 0:HALF], gt[:, 0, b, cs], ALU.mult), (tm, tbc, free["ug"][k]), s_ug)
                free["pm"][m] = tu
                t1 = q.put("gpsimd", lambda e, t=t, k=k, cs=cs: e.tensor_tensor(
                    x1[i][:, t, cs], ug[k][:, :], xi[i][:, t, cs], ALU.add), (tu, txg_[c], free["x1"][i]), s_x1)
                free["ug"][k] = t1
                if t == 3 and n2 == 1:
                    free["ah"][i] = tm
                    free["xi"][i] = t1
                    tx1[c] = t1
                yield

    def second(c):
        i, b = c % 2, c // (NCH // 2)
        rows = slice(c * CH, (c + 1) * CH)
        for t in range(4):
            for g in range(2):
                ts = q.put("vector", lambda e, t=t, g=g: e.bn_stats(
                    st[:, t, g, :], x1[i][:, t, g * HALF:(g + 1) * HALF]), (tx1[c], free["rs"]), s_st)
            ts = q.put("vector", lambda e, t=t: e.bn_aggr(mv[:, t, :], st[:, t, :, :]), (ts, free["xn"]), s_st)
        yield
        tsd = q.put("scalar", lambda e: e.activation(sd[:, :], mv[:, :, 1], ACT.Sqrt, bias=eps[:, 0:1]), (ts,), s_sd)
        trs = q.put("vector", lambda e: e.reciprocal(rs[:, :], sd[:, :]), (tsd,), s_rs)
        free["rs"] = trs
        yield
        for t in range(4):
            for a, z, d in ((0, C, 0), (512, C, C)):
                txn = q.put("vector", lambda e, t=t, a=a, z=z, d=d: e.tensor_scalar(
                    xn[:, t, d:d + z - a], x1[i][:, t, a:z], mv[:, t, 0:1], rs[:, t:t + 1], ALU.subtract, ALU.mult),
                    (trs, free["xn"]), s_xn)
            txo = q.put("gpsimd", lambda e, t=t: e.tensor_tensor(xo[:, t, :], x1[i][:, t, :], gb[:, 1, b, :], ALU.add),
                        (tx1[c], tgb, free["xo"]), s_xo)
            yield
        free["x1"][i] = txn
        free["xo"] = q.put("sync", lambda e: e.dma_start(y1[rows, :].rearrange("(t p) c -> p t c", p=128),
                                                         xo[:, :, :]), (txo,), s_y, 16)
        for kt in range(KT):
            j, k = n_pt[0] % 4, kt % 2
            n_pt[0] += 1
            for t in range(4):
                ttp = q.put("tensor", lambda e, t=t, kt=kt, j=j: e.transpose(
                    pt[j][:, t * 128:t * 128 + 128], xn[:, t, kt * 128:kt * 128 + 128], ident[:, :]),
                    (txn, free["pt"][j]), s_tp)
            thf = q.put("scalar", lambda e, kt=kt, j=j, k=k: e.activation(
                hf[k][:, :], pt[j][:, :], ACT.Identity, bias=adaT[:, 3, kt, b:b + 1], scale=adaT[:, 4, kt, b:b + 1]),
                (ttp, free["hf"][k]), s_hf)
            free["pt"][j] = thf
            thh = q.put("scalar", lambda e, kt=kt, k=k: e.activation(hh[:, kt, :], hf[k][:, :], ACT.Copy),
                        (thf, free["hh"]), s_hh)
            if kt < 4:
                thl = q.put("vector", lambda e, kt=kt, k=k: e.tensor_tensor(
                    hl[:, kt, :], hf[k][:, :], hh[:, kt, :].bitcast(F), ALU.subtract), (thh, free["hh"]), s_hl)
            else:
                thl = q.put("vector", lambda e, kt=kt, k=k: e.tensor_tensor(
                    hh[64:128, kt, :], hf[k][64:128, :], hh[64:128, kt, :].bitcast(F), ALU.subtract), (thh,), s_hl)
            free["hf"][k] = thl
            yield
        free["xn"] = ttp
        q.put("sync", lambda e: e.dma_start(hth[:, :, rows].rearrange("k p t -> p k t"), hh[:, :, :].bitcast(F)),
              (thh, thl), s_ho, 16)
        free["hh"] = q.put("sync", lambda e: e.dma_start(htl[:, :, rows].rearrange("k p t -> p k t"),
                                                         hl[:, :, :].bitcast(F)), (thl,), s_ho, 16)

    load(0)
    for _ in turn(0):
        pass
    for c in range(NCH + 1):
        if c + 1 < NCH:
            load(c + 1)
        main = project(c) if c < NCH else iter(())
        nxt = turn(c + 1) if c + 1 < NCH else iter(())
        prev = second(c - 1) if c > 0 else iter(())
        for _ in range(2):
            next(prev, None)
        for _ in main:
            next(nxt, None)
            next(prev, None)
            next(prev, None)
        for _ in nxt:
            pass
        for _ in prev:
            pass
    drain(q, s_w + s_a + s_x + [s_bc, s_y, s_ho])
    q.emit(nc)


def phase_mlp(nc, A, gd, hth, htl, y1, y2, of, W_fc1, b_fc1, W_fc2):
    NT = FF // 2 // 128
    FH = FF // 2
    q = Queues()
    wh = A.sb("wh", [128, 4, FH], R)
    wl = A.sb("wl", [128, 4, FH], R)
    wm = A.sb("wm", [128, FH], R)
    wr = A.sb("wr", [128, FH], R)
    vh = A.sb("vh", [128, NT, C], R)
    vl = A.sb("vl", [128, NT, C], R)
    stg = [A.sb(f"stg{i}", [128, FH]) for i in range(2)]
    b1 = A.sb("b1", [128, FF // 128])
    gt = A.sb("gt", [128, 2, C])
    hh = [A.sb(f"hh{i}", [128, KT, CH], R) for i in range(2)]
    hl = [A.sb(f"hl{i}", [128, 4, CH], R) for i in range(2)]
    af = [A.sb(f"af{i}", [128, CH]) for i in range(2)]
    ah = A.sb("ah", [128, NT, CH], R)
    al = A.sb("al", [128, NT, CH], R)
    yi = [A.sb(f"yi{i}", [128, C]) for i in range(2)]
    ug = [A.sb(f"ug{i}", [128, HALF]) for i in range(2)]
    pf = [A.ps(f"pf{i}", [128, 512]) for i in range(4)]
    pm = [A.ps(f"pm{i}", [128, 512]) for i in range(4)]
    s_w = [A.sem(f"w{i}") for i in range(2)]
    s_whi, s_wlo, s_z, s_c = A.sem("whi"), A.sem("wlo"), A.sem("z"), A.sem("c")
    s_h = [A.sem(f"h{i}") for i in range(2)]
    s_yi = [A.sem(f"yi{i}") for i in range(2)]
    s_yo = [A.sem(f"yo{i}") for i in range(2)]
    s_f1, s_af, s_ah, s_al, s_f2, s_ug, s_y = (A.sem("f1"), A.sem("af"), A.sem("ah"), A.sem("al"), A.sem("f2"),
                                               A.sem("ug"), A.sem("y"))
    for b in range(2):
        q.put("sync", lambda e, b=b: e.dma_start(gt[:, b, :], gd[1, b, :].partition_broadcast(128)), (), s_c, 16)
    tc = q.put("sync", lambda e: e.dma_start(b1[:, :], b_fc1.rearrange("(f p) -> p f", p=128),
                                             allow_slow_non_contiguous=True), (), s_c, 16)
    free = {"h": [None, None], "pf": [None] * 4, "pm": [None] * 4, "af": [None, None], "a": None,
            "yi": [None, None], "ug": [None, None]}
    th = {}
    n_pf, n_pm, n_ug, n_y = [0], [0], [0], [0]
    stfree = [None, None]
    mid = {}
    wrote = {}

    def load(n):
        i, c = n % 2, n % NCH
        rows = slice(c * CH, (c + 1) * CH)
        q.put("sync", lambda e: e.dma_start(hh[i][:, :, :].bitcast(F), hth[:, :, rows].rearrange("k p t -> p k t")),
              (free["h"][i],), s_h[i], 16)
        th[n] = q.put("sync", lambda e: e.dma_start(hl[i][:, :, :].bitcast(F),
                                                    htl[:, :, rows].rearrange("k p t -> p k t")),
                      (free["h"][i],), s_h[i], 16)

    def weights(half, wfree):
        for i in range(2):
            stfree[i] = stfree[i] or wfree
        if wfree is not None:
            for eng in ("scalar", "vector"):
                q.q[eng].append(([wfree], lambda e: None, None, 0))
        t1 = split_rows(q, A, W_fc1, wh, wl, wm, wr, half * FH, FH, stg, s_w, s_whi, s_wlo, s_z, stfree)
        for k in range(NT):
            i = (k + 1) % 2
            r0 = half * FH + k * 128
            ld = q.put("sync", lambda e, k=k, i=i, r0=r0: e.dma_start(stg[i][:, 0:C], W_fc2[r0:r0 + 128, :]),
                       (stfree[i],), s_w[i], 16)
            hi = q.put("scalar", lambda e, k=k, i=i: e.activation(vh[:, k, :], stg[i][:, 0:C], ACT.Copy), (ld,), s_whi)
            lo = q.put("vector", lambda e, k=k, i=i: e.tensor_tensor(
                vl[:, k, :], stg[i][:, 0:C], vh[:, k, :].bitcast(F), ALU.subtract), (ld, hi), s_wlo)
            stfree[i] = lo
        return t1, [lo, hi]

    load(0)
    for n in range(2 * NCH):
        half, c = n // NCH, n % NCH
        i, b = n % 2, c // (NCH // 2)
        if c == 0:
            tw1, tw2 = weights(half, s_f2.now() if half else None)
        if n + 1 < 2 * NCH:
            load(n + 1)
        for f in range(NT):
            m, j = n_pf[0] % 4, n_pf[0] % 2
            n_pf[0] += 1
            for k, (w, a) in enumerate(passes(wh, wl, wm, wr, hh[i], hl[i], slice(f * 128, f * 128 + 128),
                                              slice(0, CH))):
                tm = q.put("tensor", lambda e, w=w, a=a, k=k, m=m: e.matmul(
                    pf[m][:, :], w, a, start=k == 0, stop=k == 13),
                    tw1 + [th[n], free["pf"][m]], s_f1 if k == 13 else None)
            ta = q.put("scalar", lambda e, f=f, j=j, m=m, half=half: e.activation(
                af[j][:, :], pf[m][:, :], ACT.Gelu_apprx_tanh, bias=b1[:, half * NT + f:half * NT + f + 1]),
                (tm, tc, free["af"][j]), s_af)
            free["pf"][m] = ta
            tah = q.put("vector", lambda e, f=f, j=j: e.tensor_copy(ah[:, f, :], af[j][:, :]), (ta, free["a"]), s_ah)
            tal = q.put("vector", lambda e, f=f, j=j: e.tensor_tensor(
                al[:, f, :], af[j][:, :], ah[:, f, :].bitcast(F), ALU.subtract), (tah, free["a"]), s_al)
            free["af"][j] = tal
            mid[f] = [tah, tal]
        free["h"][i] = tm
        dst = y2 if half == 0 else of
        src = y1 if half == 0 else y2
        for t in range(4):
            y = n_y[0] % 2
            n_y[0] += 1
            r0 = c * CH + t * 128
            ty = q.put("sync", lambda e, y=y, r0=r0, src=src: e.dma_start(yi[y][:, :], src[r0:r0 + 128, :]),
                       (free["yi"][y], wrote.get(r0)), s_yi[y], 16)
            for n2 in range(2):
                m, k = n_pm[0] % 4, n_ug[0] % 2
                n_pm[0] += 1
                n_ug[0] += 1
                cs, ts = slice(n2 * HALF, (n2 + 1) * HALF), slice(t * 128, t * 128 + 128)
                for f in range(NT):
                    for p, (w, a) in enumerate(((ah[:, f, ts], vh[:, f, cs]), (ah[:, f, ts], vl[:, f, cs]),
                                                (al[:, f, ts], vh[:, f, cs]))):
                        end = f == NT - 1 and p == 2
                        tm = q.put("tensor", lambda e, w=w, a=a, f=f, p=p, m=m, end=end: e.matmul(
                            pm[m][:, 0:HALF], w, a, start=f == 0 and p == 0, stop=end),
                            tw2 + mid[f] + [free["pm"][m]], s_f2 if end else None)
                tu = q.put("vector", lambda e, m=m, k=k, cs=cs, b=b: e.tensor_tensor(
                    ug[k][:, :], pm[m][:, 0:HALF], gt[:, b, cs], ALU.mult), (tm, tc, free["ug"][k]), s_ug)
                free["pm"][m] = tu
                tyo = q.put("vector", lambda e, y=y, k=k, cs=cs: e.tensor_tensor(
                    yi[y][:, cs], ug[k][:, :], yi[y][:, cs], ALU.add), (tu, ty), s_y)
                free["ug"][k] = tyo
            free["yi"][y] = q.put("sync", lambda e, y=y, r0=r0, dst=dst: e.dma_start(dst[r0:r0 + 128, :],
                                                                                     yi[y][:, :]),
                                  (tyo,), s_yo[y], 16)
            wrote[r0] = free["yi"][y]
        free["a"] = tm
    drain(q, s_w + s_h + s_yi + s_yo + [s_c])
    q.emit(nc)


_INS = ["x", "cond_1152", "L0_cond_W_qkv", "L0_cond_b_qkv", "L0_cond_W_proj", "L0_cond_b_proj", "L0_cond_W_fc1",
        "L0_cond_b_fc1", "L0_cond_W_fc2", "L0_cond_b_fc2", "L0_cond_W_ada", "L0_cond_b_ada"]


def kernel(**inputs):
    import concourse.bacc as bacc
    from concourse.bass_utils import run_bass_kernel_spmd

    nc = bacc.Bacc("TRN2", target_bir_lowering=False, num_devices=1)
    arrays, args = {}, []
    for name in _INS:
        a = np.ascontiguousarray(inputs[name])
        arrays[f"in_{name}"] = a
        args.append(nc.dram_tensor(f"in_{name}", a.shape, mybir.dt.from_np(a.dtype), kind="ExternalInput").ap())
    args.append(nc.dram_tensor("out_0", (B, L, C), F, kind="ExternalOutput").ap())
    program(nc, *args)
    r = run_bass_kernel_spmd(nc, [arrays], core_ids=[0])
    return r.results[0]["out_0"]
```

```python
from contextlib import ExitStack
from itertools import chain

import numpy as np

import concourse.bass as bass
from concourse import mybir

F = mybir.dt.float32
R = mybir.dt.float32r
ALU = mybir.AluOpType
ACT = mybir.ActivationFunctionType
AX = mybir.AxisListType

B = 2
L = 2048
C = 576
H = 16
D = 36
FF = 2304
T = B * L
EPS = 1e-6
SCALE = float(D) ** -0.5
CH = 512
NCH = T // CH
KT = 5
NF = 2 * C // 128
HALF = C // 2
VW = 64 + D + 1


class Counter:

    def __init__(self, sem):
        self.sem = sem
        self.n = 0

    def now(self):
        return (self, self.n)


class Queues:

    def __init__(self):
        self.q = {e: [] for e in ("sync", "tensor", "vector", "scalar", "gpsimd")}

    def put(self, eng, fn, waits=(), inc=None, by=1):
        if inc is not None:
            inc.n += by
        self.q[eng].append(([w for w in waits if w is not None], fn, inc, by))
        return inc.now() if inc is not None else None

    def run(self, eng, e):
        seen = {}
        for waits, fn, inc, by in self.q[eng]:
            for c, v in waits:
                if v > 0 and seen.get(c, 0) < v:
                    e.wait_ge(c.sem, v)
                    seen[c] = v
            ins = fn(e)
            if inc is not None:
                ins.then_inc(inc.sem, by)

    def emit(self, nc):
        with nc.Block() as block:
            for name in self.q:
                def body(e, name=name):
                    self.run(name, e)
                blocks = {"sync": block.sync, "tensor": block.tensor, "vector": block.vector,
                                "scalar": block.scalar, "gpsimd": block.gpsimd}
                blocks[name](body)


class Scope:

    def __init__(self, nc, ctx, tag, sems):
        self.nc, self.ctx, self.tag, self.sems = nc, ctx, tag, sems

    def sb(self, name, shape, dt=F):
        return self.ctx.enter_context(self.nc.sbuf_tensor(f"{self.tag}_{name}", shape, dt))

    def ps(self, name, shape):
        return self.ctx.enter_context(self.nc.psum_tensor(f"{self.tag}_{name}", shape, F))

    def sem(self, name):
        return Counter(self.sems.enter_context(self.nc.semaphore(f"{self.tag}_s_{name}")))


def drain(q, counters):
    for c in counters:
        q.q["sync"].append(([c.now()], lambda e: None, None, 0))


def split_rows(q, s, W, wh, wl, wm, wr, c0, nc_, stg, s_ld, s_hi, s_lo, s_z, free):
    toks = []
    z = q.put("vector", lambda e: e.memset(wr[64:128, :].bitcast(F), 0.0), (), s_z)
    for kt in range(KT):
        b = kt % 2
        w = stg[b]
        if kt < 4:
            ld = q.put("sync", lambda e, kt=kt, w=w: e.dma_start(w[:, 0:nc_], W[kt * 128:kt * 128 + 128, c0:c0 + nc_]),
                       (free[b],), s_ld[b], 16)
            hi = q.put("scalar", lambda e, kt=kt, w=w: e.activation(wh[:, kt, :], w[:, 0:nc_], ACT.Copy), (ld,), s_hi)
            lo = q.put("vector", lambda e, kt=kt, w=w: e.tensor_tensor(
                wl[:, kt, :], w[:, 0:nc_], wh[:, kt, :].bitcast(F), ALU.subtract), (ld, hi), s_lo)
        else:
            q.put("sync", lambda e, w=w: e.dma_start(w[0:64, 0:nc_], W[512:576, c0:c0 + nc_]), (free[b],), s_ld[b], 16)
            ld = q.put("sync", lambda e, w=w: e.dma_start(w[64:128, 0:nc_], W[512:576, c0:c0 + nc_]), (free[b],),
                       s_ld[b], 16)
            hi = q.put("scalar", lambda e, w=w: e.activation(wm[:, :], w[:, 0:nc_], ACT.Copy), (ld,), s_hi)
            lo = q.put("vector", lambda e, w=w: e.tensor_tensor(
                wr[0:64, :], w[0:64, 0:nc_], wm[0:64, :].bitcast(F), ALU.subtract), (ld, hi), s_lo)
        free[b] = lo
        toks += [lo, hi]
    return [toks[-2], toks[-1], z]


def passes(wh, wl, wm, wr, hh, lo, wsl, tsl):
    out = []
    for kt in range(4):
        out += [(wh[:, kt, wsl], hh[:, kt, tsl]), (wh[:, kt, wsl], lo[:, kt, tsl]), (wl[:, kt, wsl], hh[:, kt, tsl])]
    out += [(wm[:, wsl], hh[:, 4, tsl]), (wr[:, wsl], hh[:, 4, tsl])]
    return out


def passes_t(wh, wl, wm, wr, hh, lo, wsl, tsl):
    out = []
    for kt in range(4):
        out += [(hh[:, kt, tsl], wh[:, kt, wsl]), (hh[:, kt, tsl], wl[:, kt, wsl]), (lo[:, kt, tsl], wh[:, kt, wsl])]
    out += [(hh[:, 4, tsl], wm[:, wsl]), (hh[:, 4, tsl], wr[:, wsl])]
    return out


def program(nc, x, cond, W_qkv, b_qkv, W_proj, b_proj, W_fc1, b_fc1, W_fc2, b_fc2, W_ada, b_ada, out):
    xf = x.rearrange("b l c -> (b l) c")
    of = out.rearrange("b l c -> (b l) c")

    def dram(name, shape):
        return nc.dram_tensor(name, shape, F, kind="Internal").ap()

    qkh = dram("qkh", [2 * C, T])
    qkl = dram("qkl", [2 * C, T])
    vd = dram("vd", [T, H * (D + 1)])
    aod = dram("aod", [T, C])
    hth = dram("hth", [KT, 128, T])
    htl = dram("htl", [4, 128, T])
    y1 = dram("y1", [T, C])
    y2 = dram("y2", [T, C])
    gd = dram("gd", [2, 2, C])

    with ExitStack() as top:
        P = Scope(nc, top, "g", top)
        ident = P.sb("ident", [128, 128])
        adaT = P.sb("adaT", [128, 6, KT, 2])
        eps = P.sb("eps", [128, 1])
        bq = P.sb("bq", [128, NF])
        sc = P.sb("sc", [128, KT, 2])
        qs0 = P.sb("qs0", [128, L], R)
        ks0 = P.sb("ks0", [128, L], R)
        mx = P.sb("mx", [128, 16, 4])

        with ExitStack() as ctx:
            A = Scope(nc, ctx, "a", top)
            wh = A.sb("wh", [128, 4, 3 * C], R)
            wl = A.sb("wl", [128, 4, 3 * C], R)
            wm = A.sb("wm", [128, 3 * C], R)
            wr = A.sb("wr", [128, 3 * C], R)
            xin = [A.sb(f"x{i}", [128, 4, C]) for i in range(2)]
            s_x = [A.sem(f"x{i}") for i in range(2)]
            phase_setup(nc, P, ident, adaT, eps, bq, sc, ks0, wh, wl, wm, wr, xin, s_x, xf, cond, W_ada, b_ada, W_qkv, b_qkv)
            phase_qkv(nc, A, ident, adaT, eps, bq, sc, qs0, ks0, mx, gd, wh, wl, wm, wr, xin, s_x, xf, W_ada,
                      b_ada, b_qkv, qkh, qkl, vd)
        with ExitStack() as ctx:
            phase_attention(nc, Scope(nc, ctx, "b", top), ident, qs0, ks0, mx, qkh, qkl, vd, aod)
        with ExitStack() as ctx:
            phase_proj(nc, Scope(nc, ctx, "c", top), ident, adaT, eps, gd, xf, aod, W_proj, b_proj, hth, htl, y1)
        with ExitStack() as ctx:
            phase_mlp(nc, Scope(nc, ctx, "d", top), gd, hth, htl, y1, y2, of, W_fc1, b_fc1, W_fc2, b_fc2)


def phase_setup(nc, P, ident, adaT, eps, bq, sc, ks0, wh, wl, wm, wr, xin, s_x, xf, cond, W_ada, b_ada, W_qkv,
                b_qkv):
    with ExitStack() as ctx:
        S = Scope(nc, ctx, "s", P.sems)
        q = Queues()
        wa = S.sb("wa", [128, KT, 2 * C])
        cT = S.sb("cT", [128, KT, 2])
        ex = S.sb("ex", [128, KT, 2])
        e1 = S.sb("e1", [128, KT, 2])
        rc = S.sb("rc", [128, KT, 2])
        bad = S.sb("bad", [2, 2, C])
        row = S.sb("row", [2, 2, 640])
        stg = [S.sb(f"stg{i}", [128, 3 * C]) for i in range(2)]
        ps = S.ps("ps", [128, 4, 512])
        s_c, s_b, s_bq = S.sem("c"), S.sem("b"), S.sem("bq")
        s_id, s_z, s_zz = S.sem("id"), S.sem("z"), S.sem("zz")
        s_wa = [S.sem(f"wa{k}") for k in range(KT)]
        s_si, s_mm, s_row, s_tr, s_ad = S.sem("si"), S.sem("mm"), S.sem("row"), S.sem("tr"), S.sem("ad")
        s_ld = [S.sem(f"ld{i}") for i in range(2)]
        s_hi, s_lo = S.sem("hi"), S.sem("lo")

        q.put("gpsimd", lambda e: e.memset(ident[:, :], 0.0), (), s_id)
        tid = q.put("gpsimd", lambda e: e.affine_select(
            out=ident[:, :], in_=ident[:, :], compare_op=ALU.not_equal, fill=1.0, base=0, pattern=[[-1, 128]],
            channel_multiplier=1), (s_id.now(),), s_id)
        zc = q.put("vector", lambda e: e.memset(cT[:, :, :], 0.0), (), s_z)
        q.put("vector", lambda e: e.memset(eps[:, :], EPS), (), s_zz)
        q.put("vector", lambda e: e.memset(ks0[96:128, :].bitcast(F), 1.0), (), s_zz)
        for b in range(2):
            q.put("sync", lambda e, b=b: e.dma_start(cT[:, 0:4, b], cond[b, 0:512].rearrange("(k p) -> p k", p=128),
                                                     allow_slow_non_contiguous=True), (zc,), s_c, 16)
            tc = q.put("sync", lambda e, b=b: e.dma_start(cT[0:64, 4, b:b + 1],
                                                          cond[b, 512:576].rearrange("(p o) -> p o", o=1),
                                                          allow_slow_non_contiguous=True), (zc,), s_c, 16)
        for kt in range(KT):
            n = 128 if kt < 4 else 64
            q.put("sync", lambda e, kt=kt, n=n: e.dma_start(wa[0:n, kt, :], W_ada[kt * 128:kt * 128 + n, 0:2 * C]), (),
                  s_wa[kt], 16)
        for b in range(2):
            tb = q.put("sync", lambda e, b=b: e.dma_start(
                bad[b:b + 1, :, :], b_ada[0:2 * C].rearrange("(o v n) -> o v n", o=1, v=2)), (), s_b, 16)
        q.put("sync", lambda e: e.dma_start(bq[:, :], b_qkv[0:2 * C].rearrange("(f p) -> p f", p=128),
                                            allow_slow_non_contiguous=True), (), s_bq, 16)

        t = q.put("scalar", lambda e: e.activation(ex[:, :, :], cT[:, :, :], ACT.Exp, scale=-1.0), (tc,), s_si)
        t = q.put("vector", lambda e: e.tensor_scalar(e1[:, :, :], ex[:, :, :], 1.0, None, ALU.add), (t,), s_si)
        t = q.put("vector", lambda e: e.reciprocal(rc[:, :, :], e1[:, :, :]), (t,), s_si)
        t = q.put("vector", lambda e: e.tensor_tensor(sc[:, :, :], cT[:, :, :], rc[:, :, :], ALU.mult), (t, tc), s_si)
        for kt in range(KT):
            n = 128 if kt < 4 else 64
            for j in range(4):
                tm = q.put("tensor", lambda e, kt=kt, n=n, j=j: e.matmul(
                    ps[0:2, j, 0:HALF], sc[0:n, kt, :], wa[0:n, kt, j * HALF:(j + 1) * HALF], start=kt == 0,
                    stop=kt == KT - 1), (t, (s_wa[kt], 16)), s_mm)
        split_rows(q, S, W_qkv, wh, wl, wm, wr, 0, 3 * C, stg, s_ld, s_hi, s_lo, s_zz, [None, None])
        q.put("sync", lambda e: e.dma_start(xin[0][:, :, :], xf[0:CH, :].rearrange("(t p) c -> p t c", p=128)), (),
              s_x[0], 16)
        for j in range(4):
            v, o = j // 2, (j % 2) * HALF
            tr = q.put("vector", lambda e, v=v, o=o, j=j: e.tensor_tensor(
                row[:, v, o:o + HALF], ps[0:2, j, 0:HALF], bad[:, v, o:o + HALF], ALU.add), (tm, tb), s_row)
        for v in range(2):
            tr = q.put("vector", lambda e, v=v: e.tensor_copy(row[:, v, C:640], row[:, v, 512:C]), (tr,), s_row)
        for v in range(2):
            for kt in range(KT):
                tt = q.put("tensor", lambda e, v=v, kt=kt: e.transpose(
                    ps[:, 0, (v * KT + kt) * 2:(v * KT + kt) * 2 + 2], row[:, v, kt * 128:kt * 128 + 128],
                    ident[0:2, 0:2]), (tr, tid), s_tr)
        ta = q.put("vector", lambda e: e.tensor_copy(adaT[:, 0:2, :, :].rearrange("p v k b -> p (v k b)"),
                                                     ps[:, 0, 0:20]), (tt,), s_ad)
        q.put("vector", lambda e: e.tensor_scalar(adaT[:, 1, :, :], adaT[:, 1, :, :], 1.0, None, ALU.add), (ta,), s_ad)
        drain(q, [s_c, s_b, s_bq, s_x[0]] + s_ld)
        q.emit(nc)


def phase_qkv(nc, A, ident, adaT, eps, bq, sc, qs0, ks0, mx, gd, wh, wl, wm, wr, xin, s_x, xf, W_ada, b_ada, b_qkv,
              qkh, qkl, vd):
    q = Queues()
    wa = A.sb("wa", [128, KT, C])
    bad = A.sb("bad", [2, C])
    row = A.sb("row", [2, 640])
    sp = [A.ps(f"sp{i}", [128, 512]) for i in range(2)]
    s_wa, s_bad, s_am, s_row, s_tr, s_ad, s_gd = (A.sem("wa"), A.sem("bad"), A.sem("am"), A.sem("row"), A.sem("tr"),
                                                  A.sem("ad"), A.sem("gd"))
    s_q0, s_s, s_mx = A.sem("q0"), A.sem("s"), A.sem("mx")
    xn = A.sb("xn", [128, 4, 640])
    st = A.sb("st", [128, 4, 2, 6])
    mv = A.sb("mv", [128, 4, 2])
    sd = A.sb("sd", [128, 4])
    rs = A.sb("rs", [128, 4])
    hf = [A.sb(f"hf{i}", [128, CH]) for i in range(2)]
    hh = [A.sb(f"hh{i}", [128, KT, CH], R) for i in range(2)]
    lo = [A.sb(f"lo{i}", [128, 4, CH], R) for i in range(2)]
    tf = [A.sb(f"tf{i}", [128, CH]) for i in range(2)]
    th = [A.sb(f"th{i}", [128, CH], R) for i in range(2)]
    tl = [A.sb(f"tl{i}", [128, CH], R) for i in range(2)]
    vc = [A.sb(f"vc{i}", [128, 4, H, D + 1]) for i in range(2)]
    bv = A.sb("bv", [128, C])
    pt = [A.ps(f"pt{i}", [128, 512]) for i in range(2)]
    pm = [A.ps(f"pm{i}", [128, 512]) for i in range(4)]
    s_bv, s_st, s_sd, s_rs, s_xn = A.sem("bv"), A.sem("st"), A.sem("sd"), A.sem("rs"), A.sem("xn")
    s_tp, s_hf, s_hh, s_lo = A.sem("tp"), A.sem("hf"), A.sem("hh"), A.sem("lo")
    s_mm, s_tf, s_tl, s_vc, s_on = A.sem("mm"), A.sem("tf"), A.sem("tl"), A.sem("vc"), A.sem("on")
    s_qo = [A.sem(f"qo{i}") for i in range(2)]
    s_vo = [A.sem(f"vo{i}") for i in range(2)]

    tbv = q.put("sync", lambda e: e.dma_start(bv[:, :], b_qkv[2 * C:3 * C].partition_broadcast(128)), (), s_bv, 16)
    for i in range(2):
        ton = q.put("vector", lambda e, i=i: e.memset(vc[i][:, :, :, D:D + 1].rearrange("p t h o -> p (t h) o"), 1.0),
                    (), s_on)
    free = {"x": [None, None], "xn": None, "pt": [None, None], "hf": [None, None], "h": [None, None],
            "pm": [None] * 4, "tf": [None, None], "tl": [None, None], "vc": [None, None], "rs": None}
    ready = {}
    tx_ = {0: s_x[0].now()}
    n_pt = [0]
    n_pm = [0]

    def load(c):
        i = c % 2
        tx_[c] = q.put("sync", lambda e: e.dma_start(
            xin[i][:, :, :], xf[c * CH:(c + 1) * CH, :].rearrange("(t p) c -> p t c", p=128)), (free["x"][i],),
            s_x[i], 16)

    def prepare(c):
        i, b = c % 2, c // (NCH // 2)
        tx = tx_[c]
        for t in range(4):
            for g in range(2):
                ts = q.put("vector", lambda e, t=t, g=g: e.bn_stats(
                    st[:, t, g, :], xin[i][:, t, g * HALF:(g + 1) * HALF]), (tx, free["rs"]), s_st)
            ts = q.put("vector", lambda e, t=t: e.bn_aggr(mv[:, t, :], st[:, t, :, :]), (ts, free["xn"]), s_st)
        tsd = q.put("scalar", lambda e: e.activation(sd[:, :], mv[:, :, 1], ACT.Sqrt, bias=eps[:, 0:1]), (ts,), s_sd)
        trs = q.put("vector", lambda e: e.reciprocal(rs[:, :], sd[:, :]), (tsd,), s_rs)
        free["rs"] = trs
        yield
        for t in range(4):
            for a, z, d in ((0, C, 0), (512, C, C)):
                txn = q.put("vector", lambda e, t=t, a=a, z=z, d=d: e.tensor_scalar(
                    xn[:, t, d:d + z - a], xin[i][:, t, a:z], mv[:, t, 0:1], rs[:, t:t + 1], ALU.subtract, ALU.mult),
                    (trs, free["xn"]), s_xn)
            if t == 1:
                yield
        free["x"][i] = txn
        if c + 1 < NCH:
            load(c + 1)
        for _ in range(3):
            yield
        for kt in range(KT):
            j = n_pt[0] % 2
            n_pt[0] += 1
            for t in range(4):
                ttp = q.put("tensor", lambda e, t=t, kt=kt, j=j: e.transpose(
                    pt[j][:, t * 128:t * 128 + 128], xn[:, t, kt * 128:kt * 128 + 128], ident[:, :]),
                    (txn, free["pt"][j]), s_tp)
            thf = q.put("scalar", lambda e, kt=kt, j=j: e.activation(
                hf[j][:, :], pt[j][:, :], ACT.Identity, bias=adaT[:, 0, kt, b:b + 1], scale=adaT[:, 1, kt, b:b + 1]),
                (ttp, free["hf"][j]), s_hf)
            free["pt"][j] = thf
            thh = q.put("vector", lambda e, kt=kt, j=j: e.tensor_copy(hh[i][:, kt, :], hf[j][:, :]),
                        (thf, free["h"][i]), s_hh)
            if kt < 4:
                tlo = q.put("vector", lambda e, kt=kt, j=j: e.tensor_tensor(
                    lo[i][:, kt, :], hf[j][:, :], hh[i][:, kt, :].bitcast(F), ALU.subtract), (thh, free["h"][i]), s_lo)
            else:
                tlo = q.put("vector", lambda e, kt=kt, j=j: e.tensor_tensor(
                    hh[i][64:128, kt, :], hf[j][64:128, :], hh[i][64:128, kt, :].bitcast(F), ALU.subtract),
                    (thh,), s_lo)
            free["hf"][j] = tlo
            yield
        free["xn"] = ttp
        ready[c] = [thh, tlo]

    def modulation():
        wfree, rfree, pfree = None, None, None
        for v in (2, 3, 4, 5):
            q.put("sync", lambda e, v=v: e.dma_start(
                wa[:, 0:4, :], W_ada[0:512, v * C:(v + 1) * C].rearrange("(k p) c -> p k c", p=128)), (wfree,), s_wa,
                16)
            tw = q.put("sync", lambda e, v=v: e.dma_start(wa[0:64, 4, :], W_ada[512:576, v * C:(v + 1) * C]),
                       (wfree,), s_wa, 16)
            for b in range(2):
                tb = q.put("sync", lambda e, v=v, b=b: e.dma_start(
                    bad[b:b + 1, :], b_ada[v * C:(v + 1) * C].rearrange("(o n) -> o n", o=1)), (rfree,), s_bad, 16)
            for _ in range(6):
                yield
            for j in range(2):
                for kt in range(KT):
                    n = 128 if kt < 4 else 64
                    tm = q.put("tensor", lambda e, kt=kt, n=n, j=j: e.matmul(
                        sp[j][0:2, 0:HALF], sc[0:n, kt, :], wa[0:n, kt, j * HALF:(j + 1) * HALF], start=kt == 0,
                        stop=kt == KT - 1), (tw, pfree), s_am)
                tr = q.put("vector", lambda e, j=j: e.tensor_tensor(
                    row[:, j * HALF:(j + 1) * HALF], sp[j][0:2, 0:HALF], bad[:, j * HALF:(j + 1) * HALF], ALU.add),
                    (tm, tb, rfree), s_row)
                yield
            wfree = tm
            tr = q.put("vector", lambda e: e.tensor_copy(row[:, C:640], row[:, 512:C]), (tr,), s_row)
            yield
            if v in (2, 5):
                rfree = q.put("sync", lambda e, v=v: e.dma_start(gd[v // 3, :, :], row[:, 0:C]), (tr,), s_gd, 16)
                pfree = tr
            else:
                for kt in range(KT):
                    tt = q.put("tensor", lambda e, kt=kt: e.transpose(
                        sp[0][:, kt * 2:kt * 2 + 2], row[:, kt * 128:kt * 128 + 128], ident[0:2, 0:2]), (tr,), s_tr)
                rfree = tt
                pfree = q.put("vector", lambda e, v=v: e.tensor_scalar(
                    adaT[:, v, :, :].rearrange("p k b -> p (k b)"), sp[0][:, 0:10], 1.0 if v == 4 else 0.0, None,
                    ALU.add), (tt,), s_ad)
            yield
        free["sp"] = [pfree, pfree]

    def first_maxima():
        stored = [c.now() for c in s_qo]
        for dst, src, r in ((qs0, qkh, 0), (qs0, qkl, 36), (qs0, qkh, 72), (ks0, qkh, 0), (ks0, qkh, 36),
                            (ks0, qkl, 72)):
            f0 = C if dst is ks0 else 0
            tl0 = q.put("sync", lambda e, dst=dst, src=src, r=r, f0=f0: e.dma_start(
                dst[r:r + D, :].bitcast(F), src[f0:f0 + D, 0:L]), stored, s_q0, 16)
        for _ in range(8):
            yield
        for n in range(64):
            qb, k4, j = n // 4, n % 4, n % 2
            t = q.put("tensor", lambda e, qb=qb, k4=k4, j=j: e.matmul(
                sp[j][:, :], qs0[0:108, qb * 128:qb * 128 + 128], ks0[0:108, k4 * 512:k4 * 512 + 512], start=True,
                stop=True), (tl0, free["sp"][j]), s_s)
            free["sp"][j] = q.put("vector", lambda e, qb=qb, k4=k4, j=j: e.tensor_reduce(
                mx[:, qb, k4:k4 + 1], sp[j][:, :], AX.X, ALU.max), (t,), s_mx)
            yield

    mod = modulation()
    top0 = None
    for _ in prepare(0):
        pass
    for c in range(NCH):
        i = c % 2
        nxt = prepare(c + 1) if c + 1 < NCH else iter(())
        if c == NCH // 2 + 1:
            for _ in mod:
                pass
            top0 = first_maxima()
        for f in range(NF):
            if top0 is None:
                next(mod, None)
            else:
                next(top0, None)
                next(top0, None)
            m, j = n_pm[0] % 4, f % 2
            n_pm[0] += 1
            ps_ = passes(wh, wl, wm, wr, hh[i], lo[i], slice(f * 128, f * 128 + 128), slice(0, CH))
            for n, (w, a) in enumerate(ps_):
                tm = q.put("tensor", lambda e, w=w, a=a, n=n, m=m: e.matmul(
                    pm[m][:, :], w, a, start=n == 0, stop=n == 13),
                    ready[c] + [free["pm"][m]], s_mm if n == 13 else None)
            tt = q.put("scalar", lambda e, f=f, j=j, m=m: e.activation(
                tf[j][:, :], pm[m][:, :], ACT.Identity, bias=bq[:, f:f + 1]), (tm, free["tf"][j]), s_tf)
            tt = q.put("scalar", lambda e, f=f, j=j, m=m: e.activation(
                th[j][:, :], pm[m][:, :], ACT.Identity, bias=bq[:, f:f + 1]), (tm, free["tl"][j]), s_tf)
            free["pm"][m] = tt
            tlw = q.put("vector", lambda e, j=j: e.tensor_tensor(
                tl[j][:, :], tf[j][:, :], th[j][:, :].bitcast(F), ALU.subtract), (tt, free["tl"][j]), s_tl)
            free["tf"][j] = tlw
            q.put("sync", lambda e, f=f, j=j, c=c: e.dma_start(
                qkh[f * 128:f * 128 + 128, c * CH:(c + 1) * CH], th[j][:, :].bitcast(F)), (tt,), s_qo[j], 16)
            free["tl"][j] = q.put("sync", lambda e, f=f, j=j, c=c: e.dma_start(
                qkl[f * 128:f * 128 + 128, c * CH:(c + 1) * CH], tl[j][:, :].bitcast(F)), (tlw,), s_qo[j], 16)
            next(nxt, None)
        for t in range(4):
            if top0 is not None:
                next(top0, None)
                next(top0, None)
            for n2 in range(2):
                m = n_pm[0] % 4
                n_pm[0] += 1
                ps_ = passes_t(wh, wl, wm, wr, hh[i], lo[i], slice(2 * C + n2 * HALF, 2 * C + (n2 + 1) * HALF),
                               slice(t * 128, t * 128 + 128))
                for n, (w, a) in enumerate(ps_):
                    tm = q.put("tensor", lambda e, w=w, a=a, n=n, m=m: e.matmul(
                        pm[m][:, 0:HALF], w, a, start=n == 0, stop=n == 13),
                        ready[c] + [free["pm"][m]], s_mm if n == 13 else None)
                tv = q.put("vector", lambda e, t=t, n2=n2, m=m, i=i: e.tensor_tensor(
                    vc[i][:, t, n2 * 8:n2 * 8 + 8, 0:D], pm[m][:, 0:HALF].rearrange("p (h d) -> p h d", d=D),
                    bv[:, n2 * HALF:(n2 + 1) * HALF].rearrange("p (h d) -> p h d", d=D), ALU.add),
                    (tm, tbv, ton, free["vc"][i]), s_vc)
                free["pm"][m] = tv
            next(nxt, None)
        free["h"][i] = tm
        free["vc"][i] = q.put("sync", lambda e, i=i, c=c: e.dma_start(
            vd[c * CH:(c + 1) * CH, :].rearrange("(t p) n -> p t n", p=128),
            vc[i][:, :, :, :].rearrange("p t h d -> p t (h d)")), (tv, ton), s_vo[i], 16)
        for _ in nxt:
            pass
    for _ in top0:
        pass
    drain(q, s_qo + s_vo + s_x + [s_bv, s_wa, s_bad, s_gd, s_q0])
    q.emit(nc)


def phase_attention(nc, A, ident, qs0, ks0, mx, qkh, qkl, vd, aod):
    q = Queues()
    NB = 3
    NH = B * H
    qs = [qs0] + [A.sb(f"qs{i}", [128, L], R) for i in range(1, NB)]
    ks = [ks0] + [A.sb(f"ks{i}", [128, L], R) for i in range(1, NB)]
    vf = [A.sb(f"vf{i}", [128, 16, D + 1]) for i in range(2)]
    vs = [A.sb(f"vs{i}", [128, 16, VW], R) for i in range(2)]
    NP = 7
    NR = 6
    pt = [A.sb(f"pt{i}", [128, 1024]) for i in range(NP)]
    ph = [A.sb(f"ph{i}", [128, 1024], R) for i in range(NR)]
    pl = [A.sb(f"pl{i}", [128, 1024], R) for i in range(NR)]
    oa = A.sb("oa", [D + 1, 1024])
    ob = A.sb("ob", [D + 1, 1024])
    oc = A.sb("oc", [D + 1, 1024])
    rc = A.sb("rc", [128, 8])
    ao = [A.sb(f"ao{i}", [128, 8, D]) for i in range(2)]
    nm = A.sb("nm", [128, 16])
    mh = A.sb("mh", [16, 128], R)
    ml = A.sb("ml", [16, 128], R)
    st = [A.ps(f"st{i}", [128, 1024]) for i in range(2)]
    op = A.ps("op", [128, 1024])
    sp = [A.ps(f"sp{i}", [128, 512]) for i in range(2)]
    s_qk = [A.sem(f"qk{i}") for i in range(NB)]
    s_v = [A.sem(f"v{i}") for i in range(2)]
    s_m = [A.sem(f"m{i}") for i in range(NB)]
    s_ao = [A.sem(f"ao{i}") for i in range(2)]
    s_one = [A.sem(f"one{i}") for i in range(NB)]
    s_ini, s_vs, s_s, s_mx, s_nm, s_mt, s_mh = (A.sem("ini"), A.sem("vs"), A.sem("s"), A.sem("mx"), A.sem("nm"),
                                                A.sem("mt"), A.sem("mh"))
    s_plg, s_phd = A.sem("plg"), A.sem("phd")
    s_st, s_p, s_ph, s_pl, s_pv = A.sem("st"), A.sem("p"), A.sem("ph"), A.sem("pl"), A.sem("pv")
    s_oe, s_oc, s_ot, s_rc, s_an = A.sem("oe"), A.sem("oc"), A.sem("ot"), A.sem("rc"), A.sem("an")

    one = [None] * NB
    zero = [None, None]

    def ones(eng, i, after):
        one[i] = q.put(eng, lambda e: e.memset(ks[i][96:128, :].bitcast(F), 1.0), (after,), s_one[i])

    def zeros(i, after):
        zero[i] = q.put("gpsimd", lambda e: e.memset(vs[i][:, :, :].bitcast(F), 0.0), (after,), s_ini)

    free = {"qk": [None] * NB, "v": [None, None], "vs": [None, None], "st": [None, None], "pt": [None] * NP,
            "ph": [None] * NR, "sp": [None, None], "op": None, "mx": None, "nm": None, "mh": None,
            "oa": None, "oc": None, "rc": None, "ao": [None, None]}
    tqk, tv, tvs, tm_ = {}, {}, {}, {}
    n_sp, n_ph = [0], [0]

    def load(h):
        i, b, hd = h % NB, h // H, h % H
        sl = slice(b * L, (b + 1) * L)
        for dst, src, r in ((qs, qkh, 0), (qs, qkl, 36), (qs, qkh, 72), (ks, qkh, 0), (ks, qkh, 36), (ks, qkl, 72)):
            f0 = hd * D + (C if dst is ks else 0)
            tqk[h] = q.put("sync", lambda e, dst=dst, src=src, r=r, f0=f0: e.dma_start(
                dst[i][r:r + D, :].bitcast(F), src[f0:f0 + D, sl]), (one[i], free["qk"][i]), s_qk[i], 16)

    def load_v(h):
        b, hd, v = h // H, h % H, h % 2
        sl = slice(b * L, (b + 1) * L)
        tv[h] = q.put("sync", lambda e: e.dma_start(
            vf[v][:, :, :],
            vd[sl, hd * (D + 1):(hd + 1) * (D + 1)].rearrange("(k p) d -> p k d", p=128)), (free["v"][v],),
            s_v[v], 16)

    def split_v(h):
        v = h % 2
        t = q.put("vector", lambda e: e.tensor_copy(vs[v][:, :, 0:D + 1], vf[v][:, :, :]),
                  (zero[v], tv[h], free["v"][v]), s_vs)
        tvs[h] = q.put("vector", lambda e: e.tensor_tensor(
            vs[v][:, :, 64:VW], vf[v][:, :, :], vs[v][:, :, 0:D + 1].bitcast(F), ALU.subtract), (t,), s_vs)

    def slot():
        j = n_sp[0] % 2
        n_sp[0] += 1
        return j

    def score_max(h, n):
        qb, k4 = n // 4, n % 4
        i, j = h % NB, slot()
        t = q.put("tensor", lambda e: e.matmul(
            sp[j][:, :], qs[i][0:108, qb * 128:qb * 128 + 128], ks[i][0:108, k4 * 512:k4 * 512 + 512], start=True,
            stop=True), (tqk[h], free["sp"][j]), s_s)
        free["sp"][j] = q.put("vector", lambda e: e.tensor_reduce(mx[:, qb, k4:k4 + 1], sp[j][:, :], AX.X, ALU.max),
                              (t, free["mx"]), s_mx)

    def row_max(h):
        t = q.put("vector", lambda e: e.tensor_reduce(nm[:, :], mx[:, :, :], AX.X, ALU.max, negate=True),
                  (s_mx.now(), free["nm"]), s_nm)
        free["mx"] = t
        return t

    def max_rows(h, t):
        i, j = h % NB, slot()
        t = q.put("tensor", lambda e: e.transpose(sp[j][0:16, 0:128], nm[:, :], ident[:, :]), (t, free["sp"][j]), s_mt)
        free["nm"] = t
        t1 = q.put("vector", lambda e: e.tensor_copy(mh[:, :], sp[j][0:16, 0:128]), (t, free["mh"]), s_mh)
        t2 = q.put("vector", lambda e: e.tensor_tensor(ml[:, :], sp[j][0:16, 0:128], mh[:, :].bitcast(F),
                                                       ALU.subtract), (t1, free["mh"]), s_mh)
        free["sp"][j] = t2
        q.put("sync", lambda e: e.dma_start(qs[i][108:109, :].bitcast(F), mh[:, :].bitcast(F)),
              (t1,), s_m[i], 16)
        tm_[h] = q.put("sync", lambda e: e.dma_start(qs[i][109:110, :].bitcast(F), ml[:, :].bitcast(F)), (t2,),
                       s_m[i], 16)
        free["mh"] = tm_[h]

    pend = {}

    def scores_t(g):
        h, u, kb = g // 32, (g // 16) % 2, g % 16
        i, j = h % NB, g % 2
        for a in range(2):
            t = q.put("tensor", lambda e, a=a: e.matmul(
                st[j][:, a * 512:a * 512 + 512], ks[i][0:110, kb * 128:kb * 128 + 128],
                qs[i][0:110, u * 1024 + a * 512:u * 1024 + a * 512 + 512], start=True, stop=True),
                (one[i], tqk[h], tm_[h], free["st"][j]), s_st if a else None)
        return t

    def exps(g, t):
        j, p = g % 2, g % NP
        tp = q.put("scalar", lambda e: e.activation(pt[p][:, :], st[j][:, :], ACT.Exp, scale=SCALE),
                   (t, free["pt"][p]), s_p)
        free["st"][j] = tp
        pend[g] = (None, tp, tp)

    def high(g):
        p, tp = g % NP, pend[g][1]
        r = n_ph[0] % NR
        n_ph[0] += 1
        if g >= G - 32 and g % 16 not in (7, 15):
            th = q.put("vector", lambda e: e.tensor_copy(ph[r][:, :], pt[p][:, :]), (tp, free["ph"][r]), s_phd)
        else:
            th = q.put("scalar", lambda e: e.activation(ph[r][:, :], pt[p][:, :], ACT.Copy), (tp, free["ph"][r]),
                       s_ph)
        pend[g] = (r, th, None)

    def low(g):
        p = g % NP
        r, th, _ = pend[g]
        pool = g % 2 == 1
        tl = q.put("gpsimd" if pool else "vector", lambda e: e.tensor_tensor(
            pl[r][:, :], pt[p][:, :], ph[r][:, :].bitcast(F), ALU.subtract), (th, free["ph"][r]),
            s_plg if pool else s_pl)
        free["pt"][p] = tl
        pend[g] = (r, th, tl)

    def pv(g):
        h, kb = g // 32, g % 16
        v = h % 2
        r, t0, t1 = pend.pop(g)
        first, last = kb == 0, kb == 15
        parts = [(vs[v][:, kb, :], ph[r], t0), (vs[v][:, kb, :], pl[r], t1)]
        for n, (w, m, tk) in enumerate(parts):
            for a in range(2):
                t = q.put("tensor", lambda e, w=w, m=m, a=a, n=n: e.matmul(
                    op[0:VW, a * 512:a * 512 + 512], w, m[:, a * 512:a * 512 + 512],
                    start=first and n == 0, stop=last and n == len(parts) - 1),
                    (tk, tvs[h], free["op"] if first else None), s_pv)
                if n == len(parts) - 1 and a == 1:
                    free["ph"][r] = t
                    if last and (g // 16) % 2 == 1:
                        free["v"][v] = t
                yield t

    def o_out(g, t):
        q.put("scalar", lambda e: e.activation(oa[:, :], op[64:VW, :], ACT.Copy), (t, free["oa"]), s_oe)
        t = q.put("scalar", lambda e: e.activation(ob[:, :], op[0:D + 1, :], ACT.Copy), (t, free["oa"]), s_oe)
        free["op"] = t
        t = q.put("gpsimd", lambda e: e.tensor_tensor(oc[:, :], oa[:, :], ob[:, :], ALU.add), (t, free["oc"]), s_oc)
        free["oa"] = t
        return t

    def o_norm(g, t):
        h, u = g // 32, (g // 16) % 2
        b, hd = h // H, h % H
        j, k = slot(), (g // 16) % 2
        for n in range(8):
            tt = q.put("tensor", lambda e, n=n: e.transpose(sp[j][:, n * 37:n * 37 + 37], oc[:, n * 128:n * 128 + 128],
                                                            ident[0:37, 0:37]), (t, free["sp"][j]), s_ot)
        free["oc"] = tt
        view = sp[j][:, 0:296].rearrange("p (n d) -> p n d", d=37)
        t1 = q.put("vector", lambda e: e.reciprocal(rc[:, :], view[:, :, D]), (tt, free["rc"]), s_rc)
        t2 = q.put("vector", lambda e: e.tensor_tensor(
            ao[k][:, :, :], view[:, :, 0:D], rc[:, :].unsqueeze(2).to_broadcast([128, 8, D]), ALU.mult),
            (t1, free["ao"][k]), s_an)
        free["sp"][j] = t2
        free["rc"] = t2
        r0 = b * L + u * 1024
        free["ao"][k] = q.put("sync", lambda e: e.dma_start(
            aod[r0:r0 + 1024, hd * D:(hd + 1) * D].rearrange("(n p) d -> p n d", p=128), ao[k][:, :, :]), (t2,),
            s_ao[k], 16)

    tqk[0] = None
    late = row_max(0)
    ones("vector", 1, None)
    zeros(0, None)
    ones("gpsimd", 2, zero[0])
    zeros(1, one[2])
    max_rows(0, late)
    load(1)
    load_v(0)
    split_v(0)
    G = NH * 32
    LAG = 5
    LEAD = 3
    todo = [64]

    def maxima(g, n, upto):
        while g > 0 and n > 0 and todo[0] < min(upto, NH * 64):
            h, k = divmod(todo[0], 64)
            score_max(h, k)
            todo[0] += 1
            n -= 1
            if k == 63:
                rows.append((h, row_max(h)))

    rows = []
    done = {}
    for g in range(G + LAG + 4):
        h, s = g // 32, g % 32
        upto = 2 * (g + 1) + 64 + 2 * LEAD
        late = rows.pop() if rows else None
        if g < G:
            if s == 0 and h + 2 < NH:
                load(h + 2)
            if h + 1 < NH and s == LAG + 1:
                load_v(h + 1)
            t = scores_t(g)
            exps(g, t)
            if g % 32 == 31:
                free["qk"][h % NB] = t
        if 0 <= g - 1 < G:
            high(g - 1)
        maxima(g, 1, upto)
        tl = None
        now = []
        if 0 <= g - LAG < G and (g - LAG) % 16 == 1:
            now.append(g - LAG - 1)
        if 0 <= g - LAG < G and (g - LAG) % 16:
            now.append(g - LAG)
        for k in now:
            for n, tl in enumerate(pv(k)):
                if n == 0:
                    maxima(g, 1, upto)
        maxima(g, 1, upto)
        if late is not None:
            max_rows(*late)
        if g in done:
            o_norm(*done.pop(g))
        if 0 <= g - 2 < G:
            low(g - 2)
        if tl is not None and (g - LAG) % 16 == 15:
            done[g + 3] = (g - LAG, o_out(g - LAG, tl))
        if g < G and h + 1 < NH and s == 16:
            split_v(h + 1)
    drain(q, s_ao + s_m + s_qk + s_v)
    q.emit(nc)


def phase_proj(nc, A, ident, adaT, eps, gd, xf, aod, W_proj, b_proj, hth, htl, y1):
    q = Queues()
    wh = A.sb("wh", [128, 4, C], R)
    wl = A.sb("wl", [128, 4, C], R)
    wm = A.sb("wm", [128, C], R)
    wr = A.sb("wr", [128, C], R)
    stg = [A.sb(f"stg{i}", [128, C]) for i in range(2)]
    gt = A.sb("gt", [128, 2, C])
    bb = A.sb("bb", [128, C])
    gb = A.sb("gb", [128, 2, C])
    ai = [A.sb(f"ai{i}", [128, 4, 640]) for i in range(2)]
    xi = [A.sb(f"xi{i}", [128, 4, C]) for i in range(2)]
    x1 = [A.sb(f"x1{i}", [128, 4, C]) for i in range(3)]
    ug = [A.sb(f"ug{i}", [128, HALF]) for i in range(2)]
    xn = [A.sb(f"xn{i}", [128, 4, 640]) for i in range(2)]
    st = [A.sb(f"st{i}", [128, 4, 2, 6]) for i in range(2)]
    mv = [A.sb(f"mv{i}", [128, 4, 2]) for i in range(2)]
    sd = [A.sb(f"sd{i}", [128, 4]) for i in range(2)]
    rs = [A.sb(f"rs{i}", [128, 4]) for i in range(2)]
    ah = [A.sb(f"ah{i}", [128, KT, CH], R) for i in range(2)]
    al = [A.sb(f"al{i}", [128, 4, CH], R) for i in range(2)]
    hf = [A.sb(f"hf{i}", [128, CH]) for i in range(2)]
    hh = A.sb("hh", [128, KT, CH], R)
    hl = A.sb("hl", [128, 4, CH], R)
    pt = [A.ps(f"pt{i}", [128, 512]) for i in range(4)]
    pm = [A.ps(f"pm{i}", [128, 512]) for i in range(4)]
    s_w = [A.sem(f"w{i}") for i in range(2)]
    s_whi, s_wlo, s_z, s_bc, s_gb = A.sem("whi"), A.sem("wlo"), A.sem("z"), A.sem("bc"), A.sem("gb")
    s_a = [A.sem(f"a{i}") for i in range(2)]
    s_x = [A.sem(f"x{i}") for i in range(2)]
    s_tp, s_ah, s_al, s_mm, s_ug, s_xg, s_x1 = (A.sem("tp"), A.sem("ah"), A.sem("al"), A.sem("mm"), A.sem("ug"),
                                                A.sem("xg"), A.sem("xa"))
    s_st, s_sd, s_rs, s_xn, s_hf, s_hh, s_hl = (A.sem("st"), A.sem("sd"), A.sem("rs"), A.sem("xn"),
                                                      A.sem("hf"), A.sem("hh"), A.sem("hl"))
    s_hs = A.sem("hs")
    s_y, s_ho = [A.sem(f"y{i}") for i in range(3)], A.sem("ho")

    tw = split_rows(q, A, W_proj, wh, wl, wm, wr, 0, C, stg, s_w, s_whi, s_wlo, s_z, [None, None])
    for b in range(2):
        q.put("sync", lambda e, b=b: e.dma_start(gt[:, b, :], gd[0, b, :].partition_broadcast(128)), (), s_bc, 16)
    tbc = q.put("sync", lambda e: e.dma_start(bb[:, :], b_proj.partition_broadcast(128)), (), s_bc, 16)
    for b in range(2):
        tgb = q.put("gpsimd", lambda e, b=b: e.tensor_tensor(gb[:, b, :], gt[:, b, :], bb[:, :], ALU.mult), (tbc,),
                    s_gb)
    free = {"ai": [None, None], "xi": [None, None], "pt": [None] * 4, "pm": [None] * 4, "ah": [None, None], "ug": [None, None],
            "x1": [None] * 3, "x1_out": [None] * 3, "xn": [None, None], "mv": [None, None], "hf": [None, None], "hh": None}
    n_pt, n_pm, n_ug = [0], [0], [0]
    tx1 = {}

    ts_, ta_, tx_, txg_, tah_, txn_ = {}, {}, {}, {}, {}, {}

    def load(c):
        i = c % 2
        rows = slice(c * CH, (c + 1) * CH)
        q.put("sync", lambda e: e.dma_start(ai[i][:, :, 0:C], aod[rows, :].rearrange("(t p) c -> p t c", p=128)),
              (free["ai"][i],), s_a[i], 16)
        ta_[c] = q.put("sync", lambda e: e.dma_start(
            ai[i][:, :, C:640], aod[rows, 512:C].rearrange("(t p) c -> p t c", p=128)), (free["ai"][i],), s_a[i], 16)

    def load_x(c):
        i = c % 2
        rows = slice(c * CH, (c + 1) * CH)
        tx = q.put("sync", lambda e: e.dma_start(xi[i][:, :, :], xf[rows, :].rearrange("(t p) c -> p t c", p=128)),
                   (free["xi"][i],), s_x[i], 16)
        tx_[c] = tx

    def add_bias(c):
        i = c % 2
        for t in range(4):
            txg_[c] = q.put("gpsimd", lambda e, t=t: e.tensor_tensor(
                xi[i][:, t, :], xi[i][:, t, :], gb[:, c // (NCH // 2), :], ALU.add), (tx_[c], tgb), s_xg)
            yield

    def turn(c):
        i = c % 2
        for kt in range(KT):
            j = n_pt[0] % 4
            n_pt[0] += 1
            for t in range(4):
                ttp = q.put("tensor", lambda e, t=t, kt=kt, j=j: e.transpose(
                    pt[j][:, t * 128:t * 128 + 128], ai[i][:, t, kt * 128:kt * 128 + 128], ident[:, :]),
                    (ta_[c], free["pt"][j]), s_tp)
            tah = q.put("scalar", lambda e, kt=kt, j=j: e.activation(ah[i][:, kt, :], pt[j][:, :], ACT.Copy),
                        (ttp, free["ah"][i]), s_ah)
            if kt < 4:
                tal = q.put("vector", lambda e, kt=kt, j=j: e.tensor_tensor(
                    al[i][:, kt, :], pt[j][:, :], ah[i][:, kt, :].bitcast(F), ALU.subtract), (tah, free["ah"][i]),
                    s_al)
            else:
                tal = q.put("vector", lambda e, kt=kt, j=j: e.tensor_tensor(
                    ah[i][64:128, kt, :], pt[j][64:128, :], ah[i][64:128, kt, :].bitcast(F), ALU.subtract), (tah,),
                    s_al)
            free["pt"][j] = tal
            if kt == KT - 1:
                free["ai"][i] = ttp
                tah_[c] = [tah, tal]
            yield

    def project(c):
        i, b, o = c % 2, c // (NCH // 2), c % 3
        for t in range(4):
            for n2 in range(2):
                m, k = n_pm[0] % 4, n_ug[0] % 2
                n_pm[0] += 1
                n_ug[0] += 1
                cs = slice(n2 * HALF, (n2 + 1) * HALF)
                for n, (w, a) in enumerate(passes_t(wh, wl, wm, wr, ah[i], al[i], cs, slice(t * 128, t * 128 + 128))):
                    tm = q.put("tensor", lambda e, w=w, a=a, n=n, m=m: e.matmul(
                        pm[m][:, 0:HALF], w, a, start=n == 0, stop=n == 13),
                        tw + tah_[c] + [free["pm"][m]], s_mm if n == 13 else None)
                tu = q.put("vector", lambda e, m=m, k=k, cs=cs: e.tensor_tensor(
                    ug[k][:, :], pm[m][:, 0:HALF], gt[:, b, cs], ALU.mult), (tm, tbc, free["ug"][k]), s_ug)
                free["pm"][m] = tu
                t1 = q.put("gpsimd", lambda e, t=t, k=k, cs=cs: e.tensor_tensor(
                    x1[o][:, t, cs], ug[k][:, :], xi[i][:, t, cs], ALU.add),
                    (tu, txg_[c], free["x1"][o], free["x1_out"][o]), s_x1)
                free["ug"][k] = t1
                tx1[c, t] = t1
                if t == 3 and n2 == 1:
                    free["ah"][i] = tm
                    free["xi"][i] = t1
                    free["x1_out"][o] = q.put("sync", lambda e: e.dma_start(
                        y1[c * CH:(c + 1) * CH, :].rearrange("(t p) c -> p t c", p=128), x1[o][:, :, :]), (t1,),
                        s_y[o], 16)
                yield

    def stats(c, t):
        i, o = c % 2, c % 3
        for g in range(2):
            ts = q.put("vector", lambda e, g=g: e.bn_stats(
                st[i][:, t, g, :], x1[o][:, t, g * HALF:(g + 1) * HALF]), (tx1[c, t], free["mv"][i]), s_st)
        ts_[c] = q.put("vector", lambda e: e.bn_aggr(mv[i][:, t, :], st[i][:, t, :, :]), (ts, free["mv"][i]), s_st)

    def norm(c, stated):
        i, o = c % 2, c % 3
        if not stated:
            for t in range(4):
                stats(c, t)
            yield
        tsd = q.put("scalar", lambda e: e.activation(sd[i][:, :], mv[i][:, :, 1], ACT.Sqrt, bias=eps[:, 0:1]),
                    (ts_[c], free["mv"][i]), s_sd)
        trs = q.put("vector", lambda e: e.reciprocal(rs[i][:, :], sd[i][:, :]), (tsd,), s_rs)
        yield
        for t in range(4):
            for a, z, d in ((0, C, 0), (512, C, C)):
                txn = q.put("vector", lambda e, t=t, a=a, z=z, d=d: e.tensor_scalar(
                    xn[i][:, t, d:d + z - a], x1[o][:, t, a:z], mv[i][:, t, 0:1], rs[i][:, t:t + 1], ALU.subtract, ALU.mult),
                    (trs, free["xn"][i]), s_xn)
            yield
        free["x1"][o] = free["mv"][i] = txn_[c] = txn

    def turn2(c):
        i, b = c % 2, c // (NCH // 2)
        rows = slice(c * CH, (c + 1) * CH)
        spare = c == NCH - 2
        oh, ol, so = (ah[i], al[i], s_hs) if spare else (hh, hl, s_ho)
        fr = free["ah"][i] if spare else free["hh"]
        for kt in range(KT):
            j, k = n_pt[0] % 4, kt % 2
            n_pt[0] += 1
            for t in range(4):
                ttp = q.put("tensor", lambda e, t=t, kt=kt, j=j: e.transpose(
                    pt[j][:, t * 128:t * 128 + 128], xn[i][:, t, kt * 128:kt * 128 + 128], ident[:, :]),
                    (txn_[c], free["pt"][j]), s_tp)
            thf = q.put("scalar", lambda e, kt=kt, j=j, k=k: e.activation(
                hf[k][:, :], pt[j][:, :], ACT.Identity, bias=adaT[:, 3, kt, b:b + 1], scale=adaT[:, 4, kt, b:b + 1]),
                (ttp, free["hf"][k]), s_hf)
            free["pt"][j] = thf
            thh = q.put("scalar", lambda e, kt=kt, k=k: e.activation(oh[:, kt, :], hf[k][:, :], ACT.Copy),
                        (thf, fr), s_hh)
            if kt < 4:
                thl = q.put("vector", lambda e, kt=kt, k=k: e.tensor_tensor(
                    ol[:, kt, :], hf[k][:, :], oh[:, kt, :].bitcast(F), ALU.subtract), (thh, fr), s_hl)
            else:
                thl = q.put("vector", lambda e, kt=kt, k=k: e.tensor_tensor(
                    oh[64:128, kt, :], hf[k][64:128, :], oh[64:128, kt, :].bitcast(F), ALU.subtract), (thh,), s_hl)
            free["hf"][k] = thl
            yield
        free["xn"][i] = ttp
        q.put("sync", lambda e: e.dma_start(hth[:, :, rows].rearrange("k p t -> p k t"), oh[:, :, :].bitcast(F)),
              (thh, thl), so, 16)
        tho = q.put("sync", lambda e: e.dma_start(htl[:, :, rows].rearrange("k p t -> p k t"),
                                                         ol[:, :, :].bitcast(F)), (thl,), so, 16)
        if not spare:
            free["hh"] = tho

    load(0)
    load_x(0)
    load(1)
    for _ in turn(0):
        pass
    for _ in add_bias(0):
        pass
    none = iter(())
    for c in range(NCH):
        end = c == NCH - 1
        if not end:
            load_x(c + 1)
        if c + 2 < NCH:
            load(c + 2)
        nxt = none if end else turn(c + 1)
        prev = norm(c - 1, False) if c > 0 else none
        old = turn2(c - 2) if c > 1 else none
        bias = none if end else add_bias(c + 1)
        for n, _ in enumerate(project(c)):
            next(nxt, None)
            next(prev, None)
            next(old, None)
            if end:
                next(prev, None)
                next(old, None)
                if n == 2:
                    for _ in chain(prev, old):
                        pass
                    old = turn2(c - 1)
                if n % 2 and n > 2:
                    stats(c, n // 2 - 1)
            elif n > 3:
                next(bias, None)
        for g in (nxt, prev, old, bias):
            for _ in g:
                pass
    stats(c, 3)
    for _ in chain(norm(c, True), turn2(c)):
        pass
    drain(q, s_w + s_a + s_x + s_y + [s_bc, s_ho, s_hs])
    q.emit(nc)


def phase_mlp(nc, A, gd, hth, htl, y1, y2, of, W_fc1, b_fc1, W_fc2, b_fc2):
    NT = FF // 2 // 128
    FH = FF // 2
    q = Queues()
    wh = A.sb("wh", [128, 4, FH], R)
    wl = A.sb("wl", [128, 4, FH], R)
    wm = A.sb("wm", [128, FH], R)
    wr = A.sb("wr", [128, FH], R)
    vh = A.sb("vh", [128, NT, C], R)
    vl = A.sb("vl", [128, NT, C], R)
    stg = [A.sb(f"stg{i}", [128, C]) for i in range(4)]
    b1 = A.sb("b1", [128, FF // 128])
    gt = A.sb("gt", [128, 2, C])
    gb = A.sb("gb", [128, 2, C])
    hh = [A.sb(f"hh{i}", [128, KT, CH], R) for i in range(2)]
    hl = [A.sb(f"hl{i}", [128, 4, CH], R) for i in range(2)]
    af = [A.sb(f"af{i}", [128, CH]) for i in range(2)]
    ah = A.sb("ah", [128, NT, CH], R)
    al = A.sb("al", [128, NT, CH], R)
    yi = [A.sb(f"yi{i}", [128, C]) for i in range(2)]
    ug = [A.sb(f"ug{i}", [128, HALF]) for i in range(2)]
    pf = [A.ps(f"pf{i}", [128, 512]) for i in range(4)]
    pm = [A.ps(f"pm{i}", [128, 512]) for i in range(4)]
    s_w = [A.sem(f"w{i}") for i in range(4)]
    s_whi, s_wlo, s_z, s_c = A.sem("whi"), A.sem("wlo"), A.sem("z"), A.sem("c")
    s_h = [A.sem(f"h{i}") for i in range(2)]
    s_gb, s_yb = A.sem("gb"), A.sem("yb")
    s_yi = [A.sem(f"yi{i}") for i in range(2)]
    s_yo = [A.sem(f"yo{i}") for i in range(2)]
    s_f1, s_af, s_ah, s_al, s_f2, s_ug, s_y = (A.sem("f1"), A.sem("af"), A.sem("ah"), A.sem("al"), A.sem("f2"),
                                               A.sem("ug"), A.sem("y"))
    free = {"h": [None, None], "pf": [None] * 4, "pm": [None] * 4, "af": [None, None], "a": None,
            "yi": [None, None], "ug": [None, None]}
    th = {}
    n_pf, n_pm, n_ug, n_y = [0], [0], [0], [0]
    stfree = [None] * 4
    n_st = [0]
    G3 = FH // 3
    tw1, tw2 = {}, {}
    mid = {}
    wrote = {}

    def load(n):
        i, c = n % 2, n % NCH
        rows = slice(c * CH, (c + 1) * CH)
        q.put("sync", lambda e: e.dma_start(hh[i][:, :, :].bitcast(F), hth[:, :, rows].rearrange("k p t -> p k t")),
              (free["h"][i],), s_h[i], 16)
        th[n] = q.put("sync", lambda e: e.dma_start(hl[i][:, :, :].bitcast(F),
                                                    htl[:, :, rows].rearrange("k p t -> p k t")),
                      (free["h"][i],), s_h[i], 16)

    def pair(src, r0, rows, c0, cols, hi_out, lo_out, wfree):
        i = n_st[0] % 4
        n_st[0] += 1
        for r in range(0, 128, rows):
            ld = q.put("sync", lambda e, r=r: e.dma_start(stg[i][r:r + rows, 0:cols],
                                                          src[r0:r0 + rows, c0:c0 + cols]), (stfree[i],), s_w[i], 16)
        hi = q.put("scalar", lambda e: e.activation(hi_out, stg[i][:, 0:cols], ACT.Copy), (ld, wfree), s_whi)
        lo = q.put("vector", lambda e: e.tensor_tensor(
            lo_out, stg[i][0:rows, 0:cols], hi_out[0:rows].bitcast(F), ALU.subtract), (ld, hi, wfree), s_wlo)
        stfree[i] = lo
        return [hi, lo]

    tz = q.put("vector", lambda e: e.memset(wr[64:128, :].bitcast(F), 0.0), (), s_z)

    def weights1(half, wfree):
        for g in range(3):
            cs = slice(g * G3, (g + 1) * G3)
            for kt in range(4):
                t = pair(W_fc1, kt * 128, 128, half * FH + g * G3, G3, wh[:, kt, cs], wl[:, kt, cs], wfree)
                yield
            tw1[g] = pair(W_fc1, 512, 64, half * FH + g * G3, G3, wm[:, cs], wr[0:64, cs], wfree) + [tz]
            yield

    def weights2(half, wfree):
        for k in range(NT):
            tw2[k] = pair(W_fc2, half * FH + k * 128, 128, 0, C, vh[:, k, :], vl[:, k, :], wfree)
            yield

    first = weights1(0, None)
    for k in range(5):
        next(first)
        if k == 2:
            load(0)
    for b in range(2):
        q.put("sync", lambda e, b=b: e.dma_start(gt[:, b, :], gd[1, b, :].partition_broadcast(128)), (), s_c, 16)
        q.put("sync", lambda e, b=b: e.dma_start(gb[:, b, :], b_fc2.partition_broadcast(128)), (), s_c, 16)
    tc = q.put("sync", lambda e: e.dma_start(b1[:, :], b_fc1.rearrange("(f p) -> p f", p=128),
                                             allow_slow_non_contiguous=True), (), s_c, 16)
    for b in range(2):
        tgb = q.put("gpsimd", lambda e, b=b: e.tensor_tensor(gb[:, b, :], gb[:, b, :], gt[:, b, :], ALU.mult), (tc,),
                    s_gb)
    for n in range(2 * NCH):
        half, c = n // NCH, n % NCH
        i, b = n % 2, c // (NCH // 2)
        gen1 = gen2 = iter(())
        if n == 0:
            for _ in first:
                pass
        if c == 0:
            gen2 = weights2(half, s_f2.now() if half else None)
        if n + 1 < 2 * NCH:
            load(n + 1)
        for f in range(NT):
            m, j = n_pf[0] % 4, n_pf[0] % 2
            n_pf[0] += 1
            for k, (w, a) in enumerate(passes(wh, wl, wm, wr, hh[i], hl[i], slice(f * 128, f * 128 + 128),
                                              slice(0, CH))):
                tm = q.put("tensor", lambda e, w=w, a=a, k=k, m=m: e.matmul(
                    pf[m][:, :], w, a, start=k == 0, stop=k == 13),
                    tw1[f // 3] + [th[n], free["pf"][m]], s_f1 if k == 13 else None)
            ta = q.put("scalar", lambda e, f=f, j=j, m=m, half=half: e.activation(
                af[j][:, :], pf[m][:, :], ACT.Gelu_apprx_tanh, bias=b1[:, half * NT + f:half * NT + f + 1]),
                (tm, tc, free["af"][j]), s_af)
            free["pf"][m] = ta
            tah = q.put("vector", lambda e, f=f, j=j: e.tensor_copy(ah[:, f, :], af[j][:, :]), (ta, free["a"]), s_ah)
            tal = q.put("vector", lambda e, f=f, j=j: e.tensor_tensor(
                al[:, f, :], af[j][:, :], ah[:, f, :].bitcast(F), ALU.subtract), (tah, free["a"]), s_al)
            free["af"][j] = tal
            mid[f] = [tah, tal]
            next(gen2, None)
        free["h"][i] = tm
        if n == NCH - 1:
            gen1 = weights1(1, tm)
        dst = y2 if half == 0 else of
        src = y1 if half == 0 else y2
        for t in range(4):
            y = n_y[0] % 2
            n_y[0] += 1
            r0 = c * CH + t * 128
            ty = q.put("sync", lambda e, y=y, r0=r0, src=src: e.dma_start(yi[y][:, :], src[r0:r0 + 128, :]),
                       (free["yi"][y], wrote.get(r0)), s_yi[y], 16)
            if half == 0:
                ty = q.put("gpsimd", lambda e, y=y, b=b: e.tensor_tensor(yi[y][:, :], yi[y][:, :], gb[:, b, :],
                                                                         ALU.add), (ty, tgb), s_yb)
            for n2 in range(2):
                m, k = n_pm[0] % 4, n_ug[0] % 2
                n_pm[0] += 1
                n_ug[0] += 1
                cs, ts = slice(n2 * HALF, (n2 + 1) * HALF), slice(t * 128, t * 128 + 128)
                for f in range(NT):
                    for p, (w, a) in enumerate(((ah[:, f, ts], vh[:, f, cs]), (ah[:, f, ts], vl[:, f, cs]),
                                                (al[:, f, ts], vh[:, f, cs]))):
                        end = f == NT - 1 and p == 2
                        tm = q.put("tensor", lambda e, w=w, a=a, f=f, p=p, m=m, end=end: e.matmul(
                            pm[m][:, 0:HALF], w, a, start=f == 0 and p == 0, stop=end),
                            tw2[f] + mid[f] + [free["pm"][m]], s_f2 if end else None)
                tu = q.put("vector", lambda e, m=m, k=k, cs=cs, b=b: e.tensor_tensor(
                    ug[k][:, :], pm[m][:, 0:HALF], gt[:, b, cs], ALU.mult), (tm, tc, free["ug"][k]), s_ug)
                free["pm"][m] = tu
                tyo = q.put("vector", lambda e, y=y, k=k, cs=cs: e.tensor_tensor(
                    yi[y][:, cs], ug[k][:, :], yi[y][:, cs], ALU.add), (tu, ty), s_y)
                free["ug"][k] = tyo
                next(gen1, None)
                next(gen1, None)
            free["yi"][y] = q.put("sync", lambda e, y=y, r0=r0, dst=dst: e.dma_start(dst[r0:r0 + 128, :],
                                                                                     yi[y][:, :]),
                                  (tyo,), s_yo[y], 16)
            wrote[r0] = free["yi"][y]
        free["a"] = tm
    drain(q, s_w + s_h + s_yi + s_yo + [s_c])
    q.emit(nc)


_INS = ["x", "cond_1152", "L0_cond_W_qkv", "L0_cond_b_qkv", "L0_cond_W_proj", "L0_cond_b_proj", "L0_cond_W_fc1",
        "L0_cond_b_fc1", "L0_cond_W_fc2", "L0_cond_b_fc2", "L0_cond_W_ada", "L0_cond_b_ada"]


def kernel(**inputs):
    import concourse.bacc as bacc
    from concourse.bass_utils import run_bass_kernel_spmd

    nc = bacc.Bacc("TRN2", target_bir_lowering=False, num_devices=1)
    arrays, args = {}, []
    for name in _INS:
        a = np.ascontiguousarray(inputs[name])
        arrays[f"in_{name}"] = a
        args.append(nc.dram_tensor(f"in_{name}", a.shape, mybir.dt.from_np(a.dtype), kind="ExternalInput").ap())
    args.append(nc.dram_tensor("out_0", (B, L, C), F, kind="ExternalOutput").ap())
    program(nc, *args)
    r = run_bass_kernel_spmd(nc, [arrays], core_ids=[0])
    return r.results[0]["out_0"]
```
